# Optimizing a Trainium2 kernel written in Bass

```python
import numpy as np
import jax
import jax.numpy as jnp

def _softmax(x, axis=-1):
    return jax.nn.softmax(x, axis=axis)

def _gelu(x):
    return jax.nn.gelu(x, approximate=True)

def _silu(x):
    return jax.nn.silu(x)

def _sigmoid(x):
    return jax.nn.sigmoid(x)

def _layernorm(x, axis=-1, eps=1e-05):
    m = jnp.mean(x, axis=axis, keepdims=True)
    v = jnp.var(x, axis=axis, keepdims=True)
    return (x - m) / jnp.sqrt(v + eps)

def _scatter_add(tgt, idx, src, axis=0):
    return tgt.at[idx].add(src)

def _segment_sum(src, seg, n):
    return jax.ops.segment_sum(src, seg, n)
kernel_name = 'mk_conv_preact_d2_conv_nchw32_r4_a6f6dc'

def setup_inputs(seed: int=0):
    np.random.seed(seed)
    _w = jnp.asarray

    def _rec_inputs():
        import jax
        import jax.numpy as jnp
        _gk = jax.random.key(seed)
        x = -0.0003482 + 1 * jax.random.normal(jax.random.fold_in(_gk, 1), (16, 32, 48, 48), jnp.float32)
        return x
    x = _rec_inputs()

    def _L0_conv_setup():
        import jax, jax.numpy as jnp
        import numpy as np
        K = 9
        PAD = 4
        N_OUT, C_IN = (32, 32)

        def _gaussian_kernels(weight, k):
            sx, sy = (weight[..., 0], weight[..., 1])
            rad = weight[..., 2] / 180.0 * jnp.pi
            c, s = (jnp.cos(rad), jnp.sin(rad))
            sx2, sy2 = (sx * sx, sy * sy)
            a = c * c * sx2 + s * s * sy2
            b = c * s * (sx2 - sy2)
            d = s * s * sx2 + c * c * sy2
            det = a * d - b * b
            ia, ib, id_ = (d / det, -b / det, a / det)
            ax = jnp.arange(k, dtype=jnp.float32) - k // 2
            xx = ax[None, :]
            yy = ax[:, None]
            q = ia[..., None, None] * (xx * xx) + 2.0 * ib[..., None, None] * (xx * yy) + id_[..., None, None] * (yy * yy)
            ker = jnp.exp(-0.5 * q)
            return ker / jnp.sum(ker, axis=(-2, -1), keepdims=True)
        key = jax.random.key(seed)
        k1, k2, k3, k4, k5 = jax.random.split(key, 5)
        x = jax.random.normal(k1, (16, C_IN, 48, 48), jnp.float32)
        sx = jax.random.uniform(k2, (N_OUT, C_IN), jnp.float32, 0.2, 4.0)
        sy = jax.random.uniform(k3, (N_OUT, C_IN), jnp.float32, 0.2, 4.0)
        th = jax.random.uniform(k4, (N_OUT, C_IN), jnp.float32, 0.0, 2.0 * np.pi)
        weight = jnp.stack([sx, sy, th], axis=-1)
        bias = jax.random.normal(k5, (N_OUT,), jnp.float32) * 0.01
        return {'x': x, 'weight': weight, 'bias': bias}
    _L0_conv_all = _L0_conv_setup()
    _L0_conv_in = {k: v for k, v in _L0_conv_all.items() if k in ('weight', 'bias')}
    del _L0_conv_all

    def _L1_conv_setup():
        import jax, jax.numpy as jnp
        import numpy as np
        key = jax.random.key(seed)
        k1, k2 = jax.random.split(key)
        x = jax.random.normal(k1, (8, 32, 63, 63), dtype=jnp.float32)
        weight = jax.random.normal(k2, (32, 32, 5, 5), dtype=jnp.float32)
        return {'x': x, 'weight': weight}
    _L1_conv_all = _L1_conv_setup()
    _L1_conv_in = {k: v for k, v in _L1_conv_all.items() if k in ('weight',)}
    del _L1_conv_all
    return {'x': x, 'L0_conv_weight': _L0_conv_in['weight'], 'L0_conv_bias': _L0_conv_in['bias'], 'L1_conv_weight': _L1_conv_in['weight']}

def reference(x, L0_conv_weight, L0_conv_bias, L1_conv_weight):
    import jax
    import jax.numpy as jnp

    def _L0_conv_ref(x, weight, bias):
        import jax, jax.numpy as jnp
        import numpy as np
        K = 9
        PAD = 4
        N_OUT, C_IN = (32, 32)

        def _gaussian_kernels(weight, k):
            sx, sy = (weight[..., 0], weight[..., 1])
            rad = weight[..., 2] / 180.0 * jnp.pi
            c, s = (jnp.cos(rad), jnp.sin(rad))
            sx2, sy2 = (sx * sx, sy * sy)
            a = c * c * sx2 + s * s * sy2
            b = c * s * (sx2 - sy2)
            d = s * s * sx2 + c * c * sy2
            det = a * d - b * b
            ia, ib, id_ = (d / det, -b / det, a / det)
            ax = jnp.arange(k, dtype=jnp.float32) - k // 2
            xx = ax[None, :]
            yy = ax[:, None]
            q = ia[..., None, None] * (xx * xx) + 2.0 * ib[..., None, None] * (xx * yy) + id_[..., None, None] * (yy * yy)
            ker = jnp.exp(-0.5 * q)
            return ker / jnp.sum(ker, axis=(-2, -1), keepdims=True)
        w = _gaussian_kernels(weight, K)
        out = jax.lax.conv_general_dilated(x, w, window_strides=(1, 1), padding=[(PAD, PAD), (PAD, PAD)], dimension_numbers=('NCHW', 'OIHW', 'NCHW'))
        return out + bias[None, :, None, None]

    def _L1_conv_ref(x, weight):
        import jax, jax.numpy as jnp
        import numpy as np
        k = weight.shape[-1]
        p = k // 2
        xp = jnp.pad(x, ((0, 0), (0, 0), (p, p), (p, p)), mode='reflect')
        H, W = (xp.shape[-2], xp.shape[-1])
        wp = jnp.zeros((weight.shape[0], weight.shape[1], H, W), dtype=x.dtype)
        wp = wp.at[:, :, :k, :k].set(weight)
        shift = -k // 2
        wp = jnp.roll(wp, shift=(shift, shift), axis=(-2, -1))
        x_fft = jnp.fft.fft2(xp)
        w_fft = jnp.fft.fft2(wp)
        out_fft = jnp.einsum('bihw,oihw->bohw', x_fft, w_fft)
        out = jnp.fft.ifft2(out_fft).real
        return out[:, :, p:-p, p:-p]

    def _gn(v, G=16, eps=1e-05):
        B_, C_, H_, W_ = v.shape
        g = v.reshape(B_, G, C_ // G, H_, W_)
        m = jnp.mean(g, axis=(2, 3, 4), keepdims=True)
        s = jnp.var(g, axis=(2, 3, 4), keepdims=True)
        return ((g - m) / jnp.sqrt(s + eps)).reshape(v.shape)

    def _ln_c(v, eps=1e-06):
        m = jnp.mean(v, axis=1, keepdims=True)
        s = jnp.var(v, axis=1, keepdims=True)
        return (v - m) / jnp.sqrt(s + eps)

    def _ln_t(v, eps=1e-05):
        m = jnp.mean(v, axis=-1, keepdims=True)
        s = jnp.var(v, axis=-1, keepdims=True)
        return (v - m) / jnp.sqrt(s + eps)

    def _to_tokens(v):
        B_, C_, H_, W_ = v.shape
        return v.reshape(B_, C_, H_ * W_).transpose(0, 2, 1)

    def _from_tokens(t, like):
        B_, C_, H_, W_ = like.shape
        return t.transpose(0, 2, 1).reshape(B_, C_, H_, W_)
    x = x + _L0_conv_ref(_gn(x), L0_conv_weight, L0_conv_bias)
    x = x + _L1_conv_ref(_gn(x), L1_conv_weight)
    return x

_drawn_inputs = setup_inputs


def setup_inputs(seed=0):
    import zlib

    import numpy as np

    out = dict(_drawn_inputs(seed))
    spreads = {}
    factors = {'L0_conv_bias': 8.0}
    for name, (base, spread) in spreads.items():
        noise = np.random.default_rng([zlib.crc32(name.encode()), seed]).standard_normal(out[name].shape)
        drawn = base * np.exp(spread * noise) if base else spread * noise
        out[name] = jnp.asarray(drawn.astype(out[name].dtype))
    for name, factor in factors.items():
        out[name] = (out[name] * factor).astype(out[name].dtype)
    return out
```

```python
from contextlib import ExitStack

import numpy as np
import concourse.bass as bass
from concourse import mybir

ALU = mybir.AluOpType
ACT = mybir.ActivationFunctionType
AX_X = mybir.AxisListType.X
F32 = mybir.dt.float32
F16 = mybir.dt.float16
BF16 = mybir.dt.bfloat16
I32 = mybir.dt.int32
RMAX = bass.bass_isa.ReduceOp.max

P = 128
B, C, H, W = 16, 32, 48, 48
RB = P // C
T = H // RB
IMG = 2
NP = B // IMG
PAIR = T * IMG * W
GROUPS = 16
N_GROUP = (C // GROUPS) * H * W
U = W // 3
OUTN = T * IMG * U
STREAMS = (1, 2, 0, 3, 4)
K1, K2 = 9, 5
PAD1 = 4
G1, G2 = 3, 2
KB1, KB2 = 3, 2
U1, U2 = U + G1 - 1, U + G2 - 1
W1 = 3 * (U1 - 1) + 5
W2 = W + 4
R1, R2 = T * IMG, (T + 1) * IMG
X_SCALE = 64.0
W1_SCALE = 4096.0
W2_SCALE = 8192.0
G_FACTOR = (0.5, -0.5, 1 / 6, 1 / 6, 1.0)
EPS = 1e-5
ROUND = 12582912.0
TWO_PI = 6.2831850
NE = KB1 * RB
SPOS = (2, 3, 4, 1, 5)
ANGLE = 5
ARGS = (38, 40, 43)
WSC = (53, 55, 58, 61, 64)
WMAX = 65
W2SCALE = 76
W2SRC = (5, 6, 0, 11, 0)
W2COUNT = (2, 4, 6, 8, 9)


def table_constants():
    kr = np.arange(P)[:, None] // C
    e = np.arange(NE)[None, :]
    yy = (RB * (e // RB) - e % RB + kr - PAD1).astype(np.float32)
    mask = np.where(np.abs(yy) <= PAD1, 0.0, -1e30).astype(np.float32)
    grp = (np.arange(P) % C) // (C // GROUPS)
    gm = (grp[:, None] == grp[None, :]).astype(np.float32) / np.float32(N_GROUP)
    return np.concatenate([yy, yy * yy, mask, gm], axis=1).astype(np.float32)


def build(nc, x, w0, bias, w1, tables, out):
    with ExitStack() as ctx:
        def sb(name, shape, dt=F32):
            return ctx.enter_context(nc.sbuf_tensor(name, shape, dt))

        def sem(name):
            return ctx.enter_context(nc.semaphore(name))

        X = sb("X", [P, NP * PAIR])
        P1 = sb("P1", [P, R1, W1])
        Z = sb("Z", [P, R2, W])
        P2 = sb("P2", [P, R2, W2])
        pre = {1: sb("pre1", [P, 4, R1 * U1]), 2: sb("pre2", [P, 4, R2 * U2])}
        s32 = {1: sb("s32_1", [P, 5, R1 * U1]), 2: sb("s32_2", [P, 5, R2 * U2])}
        SR1 = (T + 2) * IMG
        hi = {1: sb("hi1", [P, 5, SR1, U1], F16), 2: sb("hi2", [P, 5, R2, U2], F16)}
        lo = {1: sb("lo1", [P, 5, SR1, U1], F16), 2: sb("lo2", [P, 5, R2, U2], F16)}
        wh = {1: sb("wh1", [P, 5, G1 * KB1 * P], F16), 2: sb("wh2", [P, 5, G2 * KB2 * P], F16)}
        wl = {1: sb("wl1", [P, 5, G1 * KB1 * P], F16), 2: sb("wl2", [P, 5, G2 * KB2 * P], F16)}
        m1b = {1: sb("m1b1", [P, OUTN]), 2: sb("m1b2", [P, OUTN])}
        psum_ = {1: sb("ps1", [P, OUTN]), 2: sb("ps2", [P, OUTN])}
        pdif = {1: sb("pd1", [P, OUTN]), 2: sb("pd2", [P, OUTN])}
        osc = {1: sb("osc1", [P, 4]), 2: sb("osc2", [P, 4])}
        bias_c = {1: sb("bias1", [P, 1]), 2: sb("bias2", [P, 1])}
        junk = sb("junk", [P, 2, T * W], BF16)
        sums = {1: sb("sums1", [P, 4]), 2: sb("sums2", [P, 4])}
        mom = {1: sb("mom1", [P, 2, IMG]), 2: sb("mom2", [P, 2, IMG])}
        msq = {1: sb("msq1", [P, IMG]), 2: sb("msq2", [P, IMG])}
        var = {1: sb("var1", [P, IMG]), 2: sb("var2", [P, IMG])}
        vare = {1: sb("vare1", [P, IMG]), 2: sb("vare2", [P, IMG])}
        std = {1: sb("std1", [P, IMG]), 2: sb("std2", [P, IMG])}
        gsc = {1: sb("gsc1", [P, IMG]), 2: sb("gsc2", [P, IMG])}
        gof = {1: sb("gof1", [P, IMG]), 2: sb("gof2", [P, IMG])}
        tab = sb("tab", [P, 3 * NE + P])
        yy_t, yy2_t, mask_t = (tab[:, i * NE:(i + 1) * NE] for i in range(3))
        group_t = tab[:, 3 * NE:3 * NE + P]
        prm = sb("prm", [P, C, 3])
        turn = sb("turn", [P, 2, C])
        rnd = sb("rnd", [P, 2, C])
        rnd2 = sb("rnd2", [P, 2, C])
        frac = sb("frac", [P, 2, C])
        sc = sb("sc", [P, 2, C])
        scq = sb("scq", [P, 2, C])
        wq = sb("wq", [P, 2, C])
        q = sb("q", [P, 16, C])
        bt = sb("bt", [P, NE, C])
        ca = pre[2][:, :, 0:NE * C]
        ak = sb("ak", [P, 4, C])
        arg = sb("arg", [P, K1, NE * C])
        ker = arg
        gt = sb("gt", [P, 5, G1 * NE * C])
        ksum = sb("ksum", [P, C])
        krec = sb("krec", [P, C])
        rs = sb("rs", [P, 5, C])
        NW2 = KB2 * RB
        stage = sb("stage", [P, C, NW2 * K2])
        g2t = sb("g2t", [P, 8, NW2, C])
        wmax = sb("wmax", [P, 1])
        wall = sb("wall", [P, 1])
        wclamp = sb("wclamp", [P, 1])
        wpow = sb("wpow", [P, 1], I32)
        winv = sb("winv", [P, 1], I32)
        wsj = sb("wsj", [P, 4])

        banks = ctx.enter_context(nc.psum_tensor("banks", [P, 8, 512], F32))
        BANK = {1: (0, 1, 2, 3, 4), 2: (5, 6, 0, 1, 2)}
        STAT = {1: banks[:, 7, 0:4], 2: banks[:, 7, 4:8]}

        x_loaded = sem("x_loaded")
        tab_loaded = sem("tab_loaded")
        prm_loaded = sem("prm_loaded")
        stage_loaded = sem("stage_loaded")
        z_loaded = sem("z_loaded")
        stored = sem("stored")
        pads_zero = sem("pads_zero")
        stage_zero = sem("stage_zero")
        consts_set = sem("consts_set")
        sums_done = {1: sem("sums1_done"), 2: sem("sums2_done")}
        stat_mm = {1: sem("stat1_mm"), 2: sem("stat2_mm")}
        small = {1: sem("small1"), 2: sem("small2")}
        std_done = {1: sem("std1_done"), 2: sem("std2_done")}
        norm_done = {1: sem("norm1_done"), 2: sem("norm2_done")}
        pre_done = {1: sem("pre1_done"), 2: sem("pre2_done")}
        s_done = {1: sem("s1_done"), 2: sem("s2_done")}
        hi_done = {1: sem("hi1_done"), 2: sem("hi2_done")}
        lo_done = {1: sem("lo1_done"), 2: sem("lo2_done")}
        conv_mm = {1: sem("conv1_mm"), 2: sem("conv2_mm")}
        m1_read = {1: sem("m1_read1"), 2: sem("m1_read2")}
        mid_done = {1: sem("mid1_done"), 2: sem("mid2_done")}
        res_done = {1: sem("res1_done"), 2: sem("res2_done")}
        out_done = {1: sem("out1_done"), 2: sem("out2_done")}
        dve_w = sem("dve_w")
        pool_w = sem("pool_w")
        sin_done = sem("sin_done")
        exp_done = sem("exp_done")
        wh1_done = sem("wh1_done")
        wl1_done = sem("wl1_done")
        wh2_done = sem("wh2_done")
        wl2_done = sem("wl2_done")
        wmax_done = sem("wmax_done")

        def pair(n):
            return X[:, bass.ds(n * PAIR, PAIR)]

        def image(n, i):
            return pair(n).rearrange("p (t m x) -> p t m x", t=T, m=IMG)[:, :, i, :]

        def cols(n, v):
            return pair(n).rearrange("p (r u v) -> p (r u) v", u=U, v=3)[:, :, v]

        def dcol(c, k, nu):
            src = P1 if c == 1 else P2
            return src[:, :, k:k + 3 * (nu - 1) + 1:3]

        NU = {1: U1, 2: U2}
        NR = {1: R1, 2: R2}

        def f32s(c, j):
            nu = U if (c == 2 and j == 4) else NU[c]
            return s32[c][:, j, :].rearrange("p (r u) -> p r u", u=NU[c])[:, :, 0:nu]

        def pre_t(c, i, j):
            nu = U if (c == 2 and j == 4) else NU[c]
            return pre[c][:, i, :].rearrange("p (r u) -> p r u", u=NU[c])[:, :, 0:nu]

        def half(buf, c, j):
            nu = U if (c == 2 and j == 4) else NU[c]
            r0 = IMG if c == 1 else 0
            return buf[c][:, j, r0:r0 + NR[c], 0:nu]

        def tap2(k):
            return stage[:, :, :].rearrange("p o (e j) -> p e o j", j=K2)[:, :, :, K2 - 1 - k]

        def W2PARTS(j):
            return {0: ((0, tap2(0), 1), (1, tap2(3), 1)),
                    1: ((0, g2t[:, 1, :, :], 2), (1, g2t[:, 2, :, :], 2)),
                    2: ((0, g2t[:, 3, :, :], 3), (1, g2t[:, 4, :, :], 3)),
                    3: ((0, g2t[:, 7, :, :], 3), (1, g2t[:, 6, :, :], 3)),
                    4: ((0, tap2(2), 0),)}[j]

        block = ctx.enter_context(nc.Block())

        def wait(eng, s, v):
            if isinstance(v, int) and v <= 0:
                return
            eng.wait_ge(s, v)

        def addressed(eng):
            eng.nop(nofuse=True)
            eng.wait_ge(consts_set, 1)

        @block.sync
        def _(sp):
            def load(n):
                for i in range(IMG):
                    src = x[bass.ds(n * IMG + i, 1)].rearrange("b c (t k) x -> k (b c) t x", k=RB)
                    dst = image(n, i)
                    for k in range(RB):
                        sp.dma_start(dst[k * C:(k + 1) * C], src[k]).then_inc(x_loaded, 16)

            def store(n):
                sp.wait_ge(out_done[2], 5 * n + 5)
                for i in range(IMG):
                    dst = out[bass.ds(n * IMG + i, 1)].rearrange("b c (t k) x -> k (b c) t x", k=RB)
                    src = image(n, i)
                    for k in range(RB):
                        sp.dma_start(dst[k], src[k * C:(k + 1) * C]).then_inc(stored, 16)

            def shift(n):
                RW = IMG * W
                zf = Z[:, :, :].rearrange("p r x -> p (r x)")
                src = pair(n)
                sp.wait_ge(out_done[1], 5 * n + 5)
                wait(sp, norm_done[2], n)
                sp.dma_start(zf[C:P, 0:PAIR], src[0:P - C, :]).then_inc(z_loaded, 16)
                sp.dma_start(zf[0:C, RW:RW + PAIR], src[P - C:P, :]).then_inc(z_loaded, 16)
                ends = ((0, 0, 1), (1, T, H - 2), (2, T, H - 3), (3, T, 2))
                for k, t, r in ends:
                    kr, tr = r % RB, r // RB
                    sp.dma_start(zf[k * C:(k + 1) * C, t * RW:(t + 1) * RW],
                                 src[kr * C:(kr + 1) * C, tr * RW:(tr + 1) * RW]).then_inc(z_loaded, 16)

            PER = IMG * RB * 16
            load(0)
            sp.wait_ge(x_loaded, PER)
            load(1)

            def step(n, prefetch, last=False):
                if prefetch:
                    sp.wait_ge(x_loaded, PER * (n + 2))
                    load(n + 2)
                if not last:
                    shift(n)
                if not (isinstance(n, int) and n == 0):
                    store(n - 1)

            step(0, True)
            step(1, True)
            with sp.Fori(2, NP - 2) as n:
                step(n, True)
            step(NP - 2, False)
            step(NP - 1, False)
            step(NP, False, last=True)
            sp.wait_ge(stored, PER * NP)

        @block.scalar
        def _(act):
            for k in range(RB):
                act.dma_start(prm[k * C:(k + 1) * C], w0.rearrange("o c j -> c o j")).then_inc(prm_loaded, 16)
            act.dma_start(tab[:, :], tables).then_inc(tab_loaded, 16)
            for k in range(RB):
                act.dma_start(bias_c[1][k * C:(k + 1) * C, :], bias.rearrange("(o i) -> o i", i=1)).then_inc(tab_loaded, 16)
            act.wait_ge(stage_zero, 1)
            for k in range(RB):
                act.dma_start(stage[k * C:(k + 1) * C, :, k * K2:k * K2 + K2 * K2],
                              w1.rearrange("o c i j -> c o (i j)")).then_inc(stage_loaded, 16)

            def channel_sums(c, n):
                if c == 1:
                    act.wait_ge(x_loaded, IMG * RB * 16 * (n + 1))
                else:
                    act.wait_ge(out_done[1], 5 * n + 5)
                wait(act, stat_mm[c], n)
                waste = junk[:, c - 1, :].rearrange("p (t x) -> p t x", t=T)
                for i in range(2 * IMG):
                    if i == 0:
                        wait(act, sums_done[c], 2 * IMG * n)
                        addressed(act)
                    else:
                        act.wait_ge(sums_done[c], 2 * IMG * n + i)
                        addressed(act)
                    nc.scalar.activation(waste, image(n, i % IMG), (ACT.Identity, ACT.Square)[i // IMG],
                                         accum_out=sums[c][:, i:i + 1]).then_inc(sums_done[c], 1)

            def standard_deviation(c, n):
                act.wait_ge(small[c], 6 * n + 4)
                nc.scalar.activation(std[c][:, :], vare[c][:, :], ACT.Sqrt,
                                     scale=1.0 / (X_SCALE * X_SCALE)).then_inc(std_done[c], 1)

            def normalise1(n):
                act.wait_ge(small[1], 6 * n + 6)
                wait(act, s_done[1], 5 * n)
                wait(act, pre_done[1], 4 * n)
                act.wait_ge(pads_zero, 5)
                addressed(act)
                for i in range(IMG):
                    dst = P1[:, :, :].rearrange("p (t m) x -> p t m x", m=IMG)[:, :, i, PAD1:PAD1 + W]
                    nc.scalar.activation(dst, image(n, i), ACT.Identity, bias=gof[1][:, i:i + 1],
                                         scale=gsc[1][:, i:i + 1]).then_inc(norm_done[1], 1)

            def normalise2(n):
                act.wait_ge(small[2], 6 * n + 6)
                act.wait_ge(z_loaded, 6 * 16 * (n + 1))
                wait(act, s_done[2], 5 * n)
                wait(act, pre_done[2], 4 * n)
                for i in range(IMG):
                    src = Z[:, :, :].rearrange("p (t m) x -> p t m x", m=IMG)[:, :, i, :]
                    dst = P2[:, :, :].rearrange("p (t m) x -> p t m x", m=IMG)[:, :, i, :]
                    for d0, d1, ds_, s0, s1, ss in ((1, 1 + W, 1, 0, W, 1), (0, W2, W2 - 1, 1, 3, 1),
                                                    (W + 1, W + 2, 1, W - 2, W - 1, 1),
                                                    (W + 2, W + 3, 1, W - 3, W - 2, 1)):
                        ins = nc.scalar.activation(dst[:, :, d0:d1:ds_], src[:, :, s0:s1:ss], ACT.Identity,
                                                   bias=gof[2][:, i:i + 1], scale=gsc[2][:, i:i + 1])
                    ins.then_inc(norm_done[2], 1)

            def high_half(c, n, k):
                j = STREAMS[k]
                act.wait_ge(s_done[c], 5 * n + SPOS[k])
                wait(act, conv_mm[c], 5 * n + k + 1 - 5)
                nc.scalar.copy(half(hi, c, j), f32s(c, j)).then_inc(hi_done[c], 1)

            def read_m1(c, n):
                act.wait_ge(conv_mm[c], 5 * n + 1)
                wait(act, mid_done[c], 2 * n)
                nc.scalar.activation(m1b[c][:, :], banks[:, BANK[c][0], 0:OUTN], ACT.Identity,
                                     bias=bias_c[c][:, 0:1], scale=osc[c][:, 0:1]).then_inc(m1_read[c], 1)

            act.wait_ge(dve_w, ANGLE)
            nc.scalar.activation(sc[:, :, :], frac[:, :, :], ACT.Sin, scale=TWO_PI).then_inc(sin_done, 1)
            for g in range(3):
                act.wait_ge(dve_w, ARGS[g])
                nc.scalar.activation(ker[:, 3 * g:3 * g + 3, :], arg[:, 3 * g:3 * g + 3, :], ACT.Exp).then_inc(exp_done, 1)
            channel_sums(1, 0)
            standard_deviation(1, 0)
            normalise1(0)
            for k in range(5):
                high_half(1, 0, k)
            for k in range(5):
                j = STREAMS[k]
                act.wait_ge(dve_w, WSC[k])
                nc.scalar.copy(wh[1][:, j, :], gt[:, j, :]).then_inc(wh1_done, 1)
            for k in range(5):
                j = STREAMS[k]
                act.wait_ge(pool_w, W2SRC[k])
                act.wait_ge(dve_w, W2SCALE)
                for g, src, f in W2PARTS(j):
                    ins = nc.scalar.mul(wh[2][:, j, g * NW2 * C:(g + 1) * NW2 * C].rearrange("p (e o) -> p e o", o=C),
                                        src, wsj[:, f:f + 1])
                    ins.then_inc(wh2_done, 1)

            def step(n, prep, first=False, last=False):
                if not first:
                    normalise2(n - 1)
                    high_half(2, n - 1, 0)
                    high_half(2, n - 1, 1)
                if not last:
                    read_m1(1, n)
                if not first:
                    for k in range(2, 5):
                        high_half(2, n - 1, k)
                if prep:
                    channel_sums(1, n + 1)
                    standard_deviation(1, n + 1)
                    normalise1(n + 1)
                    for k in range(5):
                        high_half(1, n + 1, k)
                if not last:
                    channel_sums(2, n)
                if not first:
                    read_m1(2, n - 1)
                if not last:
                    standard_deviation(2, n)

            step(0, True, first=True)
            step(1, True)
            with act.Fori(2, NP - 1) as n:
                step(n, True)
            step(NP - 1, False)
            step(NP, False, last=True)

        @block.vector
        def _(dve):
            count = [0]

            def done(ins):
                count[0] += 1
                ins.then_inc(dve_w, 1)

            def stage_end():
                dve.wait_ge(dve_w, count[0])

            tt, ts, stt = nc.vector.tensor_tensor, nc.vector.tensor_scalar, nc.vector.scalar_tensor_tensor

            def angles():
                dve.wait_ge(prm_loaded, 16 * RB)
                done(ts(turn[:, 0, :], prm[:, :, 2], 1.0 / 360.0, None, ALU.mult))
                done(ts(turn[:, 1, :], prm[:, :, 2], 1.0 / 360.0, 0.25, ALU.mult, ALU.add))
                stage_end()
                done(ts(rnd[:, :, :], turn[:, :, :], ROUND, None, ALU.add))
                stage_end()
                done(ts(rnd2[:, :, :], rnd[:, :, :], -ROUND, None, ALU.add))
                stage_end()
                done(tt(frac[:, :, :], turn[:, :, :], rnd2[:, :, :], ALU.subtract))
                assert count[0] == ANGLE

            def exponents():
                mul = ALU.mult
                done(tt(wq[:, 0, :], prm[:, :, 0], prm[:, :, 0], mul))
                done(tt(wq[:, 1, :], prm[:, :, 1], prm[:, :, 1], mul))
                dve.wait_ge(sin_done, 1)
                done(tt(scq[:, :, :], sc[:, :, :], sc[:, :, :], mul))
                done(tt(q[:, 0, :], sc[:, 0, :], sc[:, 1, :], mul))
                stage_end()
                done(tt(q[:, 1, :], scq[:, 1, :], wq[:, 0, :], mul))
                done(tt(q[:, 2, :], scq[:, 0, :], wq[:, 1, :], mul))
                done(tt(q[:, 3, :], scq[:, 0, :], wq[:, 0, :], mul))
                done(tt(q[:, 4, :], scq[:, 1, :], wq[:, 1, :], mul))
                done(tt(q[:, 5, :], wq[:, 0, :], wq[:, 1, :], ALU.subtract))
                stage_end()
                done(tt(q[:, 6, :], q[:, 1, :], q[:, 2, :], ALU.add))
                done(tt(q[:, 7, :], q[:, 3, :], q[:, 4, :], ALU.add))
                done(tt(q[:, 8, :], q[:, 0, :], q[:, 5, :], mul))
                stage_end()
                done(tt(q[:, 9, :], q[:, 6, :], q[:, 7, :], mul))
                done(tt(q[:, 10, :], q[:, 8, :], q[:, 8, :], mul))
                stage_end()
                done(tt(q[:, 11, :], q[:, 9, :], q[:, 10, :], ALU.subtract))
                stage_end()
                done(nc.vector.reciprocal(q[:, 12, :], q[:, 11, :]))
                stage_end()
                done(stt(q[:, 13, :], q[:, 7, :], -0.5, q[:, 12, :], mul, mul))
                done(tt(q[:, 14, :], q[:, 8, :], q[:, 12, :], mul))
                done(stt(q[:, 15, :], q[:, 6, :], -0.5, q[:, 12, :], mul, mul))
                stage_end()
                dve.wait_ge(tab_loaded, 16 * 5)

                def rows(v):
                    return v.unsqueeze(2).to_broadcast([P, NE, C])

                def chans(v):
                    return v.unsqueeze(1).to_broadcast([P, NE, C])

                cc = arg[:, PAD1, :].rearrange("p (e o) -> p e o", o=C)
                done(tt(cc, rows(yy2_t), chans(q[:, 15, :]), mul))
                done(tt(bt[:, :, :], rows(yy_t), chans(q[:, 14, :]), mul))
                for k in range(1, 5):
                    done(ts(ak[:, k - 1, :], q[:, 13, :], float(k * k), None, mul))
                stage_end()
                done(tt(cc, cc, rows(mask_t), ALU.add))
                stage_end()
                for k in range(1, 5):
                    done(tt(ca[:, k - 1, :].rearrange("p (e o) -> p e o", o=C), cc, chans(ak[:, k - 1, :]), ALU.add))
                stage_end()
                btf = bt[:, :, :].rearrange("p e o -> p (e o)")
                marks = []
                for t in range(K1):
                    k = t - PAD1
                    if k != 0:
                        done(stt(arg[:, t, :], btf, float(k), ca[:, abs(k) - 1, :], mul, ALU.add))
                    if t % 3 == 2:
                        marks.append(count[0])
                assert tuple(marks) == ARGS, marks

            def tap(k):
                return ker[:, :, :].rearrange("p (g k) e -> p g k e", k=3)[:, :, k, :]

            def gtv(i):
                return gt[:, i, :].rearrange("p (g e) -> p g e", g=G1)

            def kernel_streams():
                mul = ALU.mult
                dve.wait_ge(exp_done, 3)
                done(tt(gtv(0), tap(0), tap(2), ALU.add))
                stage_end()
                done(tt(gtv(1), gtv(0), tap(1), ALU.add))
                stage_end()
                done(nc.vector.tensor_reduce(ksum[:, :], gt[:, 1, :].rearrange("p (r o) -> p o r", o=C), AX_X, ALU.add))
                stage_end()
                done(nc.vector.reciprocal(krec[:, :], ksum[:, :]))
                stage_end()
                for j in range(5):
                    done(ts(rs[:, j, :], krec[:, :], W1_SCALE * G_FACTOR[j], None, mul))
                stage_end()
                marks = []
                for k in range(5):
                    j = STREAMS[k]
                    if j == 2:
                        done(tt(gtv(2), tap(1), gtv(0), ALU.subtract))
                        stage_end()
                    if j == 3:
                        done(stt(gtv(4), tap(1), 2.0, tap(0), mul, ALU.add))
                        stage_end()
                        done(stt(gtv(3), tap(2), 4.0, gtv(4), mul, ALU.add))
                        stage_end()
                    src = {0: tap(0), 4: tap(2)}.get(j)
                    if src is None:
                        done(tt(gt[:, j, :].rearrange("p (r o) -> p r o", o=C),
                                gt[:, j, :].rearrange("p (r o) -> p r o", o=C),
                                rs[:, j, :].unsqueeze(1).to_broadcast([P, G1 * NE, C]), mul))
                    else:
                        for g in range(G1):
                            done(tt(gt[:, j, g * NE * C:(g + 1) * NE * C].rearrange("p (e o) -> p e o", o=C),
                                    src[:, g, :].rearrange("p (e o) -> p e o", o=C),
                                    rs[:, j, :].unsqueeze(1).to_broadcast([P, NE, C]), mul))
                    marks.append(count[0])
                    if k > 0:
                        low_kernel(k - 1)
                low_kernel(4)
                assert tuple(marks) == WSC, marks

            def low_kernel(k):
                j = STREAMS[k]
                dve.wait_ge(wh1_done, k + 1)
                tt(wl[1][:, j, :], gt[:, j, :], wh[1][:, j, :], ALU.subtract).then_inc(wl1_done, 1)

            def layer2_scale():
                dve.wait_ge(stage_loaded, 16 * RB)
                done(nc.vector.tensor_reduce(wmax[:, :], stage[:, :, :].rearrange("p o e -> p (o e)"), AX_X, ALU.max,
                                             apply_absolute_value=True))
                assert count[0] == WMAX
                dve.wait_ge(wmax_done, 1)
                done(ts(wclamp[:, :], wall[:, :], 1e-30, None, ALU.max))
                stage_end()
                done(ts(wpow[:, :], wclamp[:, :].bitcast(I32), 0x7F800000, None, ALU.bitwise_and))
                stage_end()
                done(ts(winv[:, :], wpow[:, :], -1.0, float(0x7F000000), ALU.mult, ALU.add))
                for f, v in enumerate((1.0, -1.0, 2.0, 4.0)):
                    done(ts(osc[2][:, f:f + 1], wpow[:, :].bitcast(F32), v / (X_SCALE * W2_SCALE), None, ALU.mult))
                stage_end()
                for f, v in enumerate((1.0, 0.5, -0.5, 1 / 6)):
                    done(ts(wsj[:, f:f + 1], winv[:, :].bitcast(F32), v * W2_SCALE, None, ALU.mult))
                stage_end()
                assert count[0] == W2SCALE, count[0]

            def low_layer2():
                m = 0
                for k in range(5):
                    j = STREAMS[k]
                    dve.wait_ge(pool_w, W2SRC[k])
                    for g, src, f in W2PARTS(j):
                        m += 1
                        dve.wait_ge(wh2_done, m)
                        sl = slice(g * NW2 * C, (g + 1) * NW2 * C)
                        stt(wl[2][:, j, sl].rearrange("p (e o) -> p e o", o=C), src, wsj[:, f:f + 1],
                            wh[2][:, j, sl].rearrange("p (e o) -> p e o", o=C), ALU.mult, ALU.subtract).then_inc(wl2_done, 1)

            def small_stats(c, n):
                dve.wait_ge(stat_mm[c], n + 1)
                wait(dve, norm_done[c], IMG * n)
                nc.vector.tensor_copy(mom[c][:, :, :].rearrange("p a b -> p (a b)"), STAT[c]).then_inc(small[c], 1)
                mean, ex2 = mom[c][:, 0, :], mom[c][:, 1, :]
                dve.wait_ge(small[c], 6 * n + 1)
                stt(msq[c][:, :], mean, -1.0, mean, ALU.mult, ALU.mult).then_inc(small[c], 1)
                dve.wait_ge(small[c], 6 * n + 2)
                tt(var[c][:, :], ex2, msq[c][:, :], ALU.add).then_inc(small[c], 1)
                dve.wait_ge(small[c], 6 * n + 3)
                ts(vare[c][:, :], var[c][:, :], 0.0, EPS, ALU.max, ALU.add).then_inc(small[c], 1)
                dve.wait_ge(std_done[c], n + 1)
                nc.vector.reciprocal(gsc[c][:, :], std[c][:, :]).then_inc(small[c], 1)
                dve.wait_ge(small[c], 6 * n + 5)
                stt(gof[c][:, :], mean, -1.0, gsc[c][:, :], ALU.mult, ALU.mult).then_inc(small[c], 1)

            def make_stream(c, n, k):
                j = (3, 1, 2, 0, 4)[k]
                if k == 0:
                    dve.wait_ge(norm_done[c], IMG * (n + 1))
                    tt(f32s(c, 3), dcol(c, 3, NU[c]), dcol(c, 1, NU[c]), ALU.subtract).then_inc(s_done[c], 1)
                    return
                dve.wait_ge(pre_done[c], 4 * n + k)
                if k == 1:
                    dve.wait_ge(s_done[c], 5 * n + 1)
                nu = U if (c == 2 and j == 4) else NU[c]
                a = f32s(c, 3)[:, :, 0:nu]
                t_ = pre_t(c, k - 1, j)
                if j == 1:
                    tt(f32s(c, 1), a, t_, ALU.subtract).then_inc(s_done[c], 1)
                elif j == 2:
                    stt(f32s(c, 2), t_, 3.0, a, ALU.mult, ALU.add).then_inc(s_done[c], 1)
                elif j == 0:
                    stt(f32s(c, 0), t_, 2.0, a, ALU.mult, ALU.add).then_inc(s_done[c], 1)
                else:
                    stt(f32s(c, 4), a, -2.0, t_, ALU.mult, ALU.add).then_inc(s_done[c], 1)

            def low_half(c, n, k):
                j = STREAMS[k]
                dve.wait_ge(hi_done[c], 5 * n + k + 1)
                tt(half(lo, c, j), f32s(c, j), half(hi, c, j), ALU.subtract).then_inc(lo_done[c], 1)

            def product(c, k):
                return banks[:, BANK[c][k], 0:OUTN]

            def middle(c, n):
                dve.wait_ge(conv_mm[c], 5 * n + 2)
                dve.wait_ge(m1_read[c], n + 1)
                wait(dve, res_done[c], 3 * n)
                stt(psum_[c][:, :], product(c, 1), osc[c][:, 0:1], m1b[c][:, :], ALU.mult, ALU.add).then_inc(mid_done[c], 1)
                stt(pdif[c][:, :], product(c, 1), osc[c][:, 1:2], m1b[c][:, :], ALU.mult, ALU.add).then_inc(mid_done[c], 1)

            def add_m0(c, n):
                dve.wait_ge(conv_mm[c], 5 * n + 3)
                dve.wait_ge(res_done[c], 3 * n + 1)
                stt(cols(n, 0), product(c, 2), osc[c][:, 0:1], cols(n, 0), ALU.mult, ALU.add).then_inc(out_done[c], 1)

            def add_m3(c, n):
                dve.wait_ge(conv_mm[c], 5 * n + 4)
                dve.wait_ge(res_done[c], 3 * n + 3)
                stt(cols(n, 1), product(c, 3), osc[c][:, 2:3], cols(n, 1), ALU.mult, ALU.add).then_inc(out_done[c], 1)
                stt(cols(n, 2), product(c, 3), osc[c][:, 3:4], cols(n, 2), ALU.mult, ALU.add).then_inc(out_done[c], 1)
                dve.wait_ge(out_done[c], 5 * n + 1)
                stt(cols(n, 0), product(c, 3), osc[c][:, 0:1], cols(n, 0), ALU.mult, ALU.add).then_inc(out_done[c], 1)

            def add_m4(c, n):
                dve.wait_ge(conv_mm[c], 5 * n + 5)
                dve.wait_ge(out_done[c], 5 * n + 3)
                stt(cols(n, 2), product(c, 4), osc[c][:, 0:1], cols(n, 2), ALU.mult, ALU.add).then_inc(out_done[c], 1)

            angles()
            exponents()
            small_stats(1, 0)
            for k in range(5):
                make_stream(1, 0, k)
            for k in range(5):
                low_half(1, 0, k)
            kernel_streams()
            layer2_scale()
            low_layer2()
            dve.wait_ge(consts_set, 1)

            def step(n, prep, first=False, last=False):
                if not first:
                    for k in range(5):
                        make_stream(2, n - 1, k)
                    for k in range(5):
                        low_half(2, n - 1, k)
                if prep:
                    small_stats(1, n + 1)
                if not last:
                    middle(1, n)
                if prep:
                    for k in range(5):
                        make_stream(1, n + 1, k)
                    for k in range(2):
                        low_half(1, n + 1, k)
                if not last:
                    add_m0(1, n)
                if prep:
                    low_half(1, n + 1, 2)
                if not last:
                    add_m3(1, n)
                if prep:
                    low_half(1, n + 1, 3)
                if not last:
                    add_m4(1, n)
                if prep:
                    low_half(1, n + 1, 4)
                if not first:
                    middle(2, n - 1)
                    add_m0(2, n - 1)
                if not last:
                    small_stats(2, n)
                if not first:
                    add_m3(2, n - 1)
                    add_m4(2, n - 1)

            step(0, True, first=True)
            step(1, True)
            with dve.Fori(2, NP - 1) as n:
                step(n, True)
            step(NP - 1, False)
            step(NP, False, last=True)

        @block.gpsimd
        def _(pool):
            nc.gpsimd.memset(stage[:, :, :], 0.0).then_inc(stage_zero, 1)
            nc.gpsimd.memset(P1[:, :, :], 0.0).then_inc(pads_zero, 1)
            for buf in (hi[1], lo[1]):
                nc.gpsimd.memset(buf[:, :, 0:IMG, :], 0.0).then_inc(pads_zero, 1)
                nc.gpsimd.memset(buf[:, :, IMG + R1:, :], 0.0).then_inc(pads_zero, 1)
            for f, v in enumerate((1.0, -1.0, 2.0, 4.0)):
                nc.gpsimd.memset(osc[1][:, f:f + 1], v / (X_SCALE * W1_SCALE))
            nc.gpsimd.memset(bias_c[2][:, :], 0.0).then_inc(consts_set, 1)

            tt, ts = nc.gpsimd.tensor_tensor, nc.gpsimd.tensor_scalar
            count = [0]

            def done(ins):
                count[0] += 1
                ins.then_inc(pool_w, 1)

            def stage_end():
                pool.wait_ge(pool_w, count[0])

            def layer2_taps():
                marks = [0] * 5
                done(tt(g2t[:, 0, :, :], tap2(0), tap2(2), ALU.add))
                done(tt(g2t[:, 2, :, :], tap2(3), tap2(4), ALU.add))
                done(tt(g2t[:, 4, :, :], tap2(4), tap2(3), ALU.subtract))
                done(ts(g2t[:, 7, :, :], tap2(1), 2.0, None, ALU.mult))
                stage_end()
                done(tt(g2t[:, 1, :, :], g2t[:, 0, :, :], tap2(1), ALU.add))
                done(tt(g2t[:, 3, :, :], tap2(1), g2t[:, 0, :, :], ALU.subtract))
                stage_end()
                done(tt(g2t[:, 5, :, :], g2t[:, 7, :, :], tap2(0), ALU.add))
                done(ts(g2t[:, 0, :, :], tap2(2), 4.0, None, ALU.mult))
                stage_end()
                done(tt(g2t[:, 7, :, :], g2t[:, 5, :, :], g2t[:, 0, :, :], ALU.add))
                stage_end()
                done(ts(g2t[:, 5, :, :], tap2(4), 2.0, None, ALU.mult))
                stage_end()
                done(tt(g2t[:, 6, :, :], g2t[:, 5, :, :], tap2(3), ALU.add))
                assert count[0] == W2SRC[3], count[0]

            def pre_sums(c, n):
                pool.wait_ge(norm_done[c], IMG * (n + 1))
                terms = ((1, 2, ALU.add, 1), (1, 2, ALU.subtract, 2), (0, 2, ALU.subtract, 0), (4, 2, ALU.subtract, 4))
                for i, (a, b, op, j) in enumerate(terms):
                    nu = U if (c == 2 and j == 4) else NU[c]
                    if i == 0:
                        wait(pool, s_done[c], 5 * n)
                    tt(pre_t(c, i, j), dcol(c, a, nu), dcol(c, b, nu), op).then_inc(pre_done[c], 1)

            def residual(c, n):
                for i, (v, src) in enumerate(((0, psum_), (1, pdif), (2, psum_))):
                    if i == 0:
                        pool.wait_ge(mid_done[c], 2 * n + 1)
                        if c == 1:
                            pool.wait_ge(norm_done[1], IMG * (n + 1))
                        else:
                            pool.wait_ge(z_loaded, 6 * 16 * (n + 1))
                            pool.wait_ge(sums_done[2], 2 * IMG * (n + 1))
                    if i == 1:
                        pool.wait_ge(mid_done[c], 2 * n + 2)
                    addressed(pool)
                    tt(cols(n, v), cols(n, v), src[c][:, :], ALU.add).then_inc(res_done[c], 1)

            pool.wait_ge(pads_zero, 5)
            pool.wait_ge(norm_done[1], IMG)
            pre_sums(1, 0)
            pool.wait_ge(dve_w, WMAX)
            nc.gpsimd.partition_all_reduce(wall[:, :], wmax[:, :], P, RMAX).then_inc(wmax_done, 1)
            layer2_taps()

            def step(n, prep, first=False, last=False):
                if not first:
                    pre_sums(2, n - 1)
                if prep:
                    pre_sums(1, n + 1)
                if not last:
                    residual(1, n)
                if not first:
                    residual(2, n - 1)

            step(0, True, first=True)
            step(1, True)
            with pool.Fori(2, NP - 1) as n:
                step(n, True)
            step(NP - 1, False)
            step(NP, False, last=True)

        @block.tensor
        def _(pe):
            KB = {1: KB1, 2: KB2}
            G = {1: G1, 2: G2}

            def stats(c, n):
                pe.wait_ge(sums_done[c], 2 * IMG * (n + 1))
                nc.tensor.matmul(STAT[c], group_t, sums[c][:, :], start=True, stop=True).then_inc(stat_mm[c], 1)

            def conv_stream(c, n, k):
                j = STREAMS[k]
                pe.wait_ge(hi_done[c], 5 * n + k + 1)
                pe.wait_ge(lo_done[c], 5 * n + k + 1)
                groups = 1 if (c == 2 and j == 4) else G[c]
                steps = [(g, b) for g in range(groups) for b in range(KB[c])]
                for i, (g, b) in enumerate(steps):
                    if c == 1:
                        at = (g * KB1 + b) * P
                    else:
                        at = (g * KB2 + KB2 - 1 - b) * P
                    high, low = wh[c][:, j, at:at + P], wl[c][:, j, at:at + P]
                    xh = hi[c][:, j, IMG * b:IMG * b + T * IMG, g:g + U]
                    xl = lo[c][:, j, IMG * b:IMG * b + T * IMG, g:g + U]
                    dst = banks[:, BANK[c][k], 0:OUTN].rearrange("p (r u) -> p r u", u=U)
                    nc.tensor.matmul(dst, high, xh, start=(i == 0), stop=False)
                    nc.tensor.matmul(dst, high, xl, start=False, stop=False)
                    ins = nc.tensor.matmul(dst, low, xh, start=False, stop=(i == len(steps) - 1))
                ins.then_inc(conv_mm[c], 1)

            def bank_free(c, n, k, final=False):
                if c == 1:
                    if k < 3:
                        wait(pe, out_done[2], 5 * (n - 2) + (1, 4, 5)[k])
                        if isinstance(n, int) and n == 1:
                            pe.wait_ge(*((m1_read[1], 1), (mid_done[1], 2), (out_done[1], 1))[k])
                    else:
                        wait(pe, out_done[1], 5 * (n - 1) + (4, 5)[k - 3])
                elif k == 0:
                    wait(pe, m1_read[2], n)
                elif k == 1:
                    wait(pe, mid_done[2], 2 * n)
                elif final:
                    pe.wait_ge(out_done[2], 5 * (n - 1) + (1, 4, 5)[k - 2])
                elif k == 2:
                    pe.wait_ge(m1_read[1], n + 2)
                elif k == 3:
                    pe.wait_ge(mid_done[1], 2 * (n + 2))
                else:
                    pe.wait_ge(out_done[1], 5 * (n + 1) + 1)

            def step(n, prep, first=False, last=False):
                if not last:
                    for k in range(5):
                        if first:
                            pe.wait_ge(wh1_done, k + 1)
                            pe.wait_ge(wl1_done, k + 1)
                        bank_free(1, n, k)
                        conv_stream(1, n, k)
                        if k == 0 and isinstance(n, int) and n == 1:
                            stats(2, 0)
                        if k == 1 and prep:
                            stats(1, n + 1)
                if not first:
                    for k in range(5):
                        if isinstance(n, int) and n == 1:
                            parts = W2COUNT[k]
                            pe.wait_ge(wh2_done, parts)
                            pe.wait_ge(wl2_done, parts)
                        bank_free(2, n - 1, k, final=last)
                        conv_stream(2, n - 1, k)
                        if k == 2 and not last:
                            stats(2, n)

            pe.wait_ge(tab_loaded, 16 * 5)
            pe.wait_ge(pads_zero, 5)
            stats(1, 0)
            step(0, True, first=True)
            step(1, True)
            with pe.Fori(2, NP - 1) as n:
                step(n, True)
            step(NP - 1, False)
            step(NP, False, last=True)


def kernel(x, L0_conv_weight, L0_conv_bias, L1_conv_weight):
    import concourse.bacc as bacc
    from concourse.bass_utils import run_bass_kernel_spmd

    nc = bacc.Bacc("TRN2", target_bir_lowering=False, num_devices=1)
    arrays = {
        "x": np.ascontiguousarray(x),
        "w0": np.ascontiguousarray(L0_conv_weight),
        "bias": np.ascontiguousarray(L0_conv_bias),
        "w1": np.ascontiguousarray(L1_conv_weight),
        "tables": table_constants(),
    }
    args = [nc.dram_tensor(f"in_{k}", a.shape, mybir.dt.from_np(a.dtype), kind="ExternalInput").ap()
            for k, a in arrays.items()]
    out = nc.dram_tensor("out", (B, C, H, W), F32, kind="ExternalOutput").ap()
    build(nc, *args, out)
    r = run_bass_kernel_spmd(nc, [{f"in_{k}": a for k, a in arrays.items()}], core_ids=[0])
    return r.results[0]["out"]
```

```python
from contextlib import ExitStack

import numpy as np
import concourse.bass as bass
from concourse import mybir

ALU = mybir.AluOpType
ACT = mybir.ActivationFunctionType
AX_X = mybir.AxisListType.X
F32 = mybir.dt.float32
F16 = mybir.dt.float16
BF16 = mybir.dt.bfloat16
I32 = mybir.dt.int32
RMAX = bass.bass_isa.ReduceOp.max

P = 128
B, C, H, W = 16, 32, 48, 48
RB = P // C
T = H // RB
IMG = 2
NP = B // IMG
PAIR = T * IMG * W
GROUPS = 16
N_GROUP = (C // GROUPS) * H * W
U = W // 3
OUTN = T * IMG * U
STREAMS = (1, 2, 0, 3, 4)
K1, K2 = 9, 5
PAD1 = 4
G1, G2 = 3, 2
KB1, KB2 = 3, 2
U1, U2 = U + G1 - 1, U + G2 - 1
W1 = 3 * (U1 - 1) + 5
W2 = W + 4
R1, R2 = T * IMG, (T + 1) * IMG
X_SCALE = 64.0
W1_SCALE = 4096.0
W2_SCALE = 8192.0
G_FACTOR = (0.5, -0.5, 1 / 6, 1 / 6, 1.0)
EPS = 1e-5
ROUND = 12582912.0
TWO_PI = 6.2831850
NE = KB1 * RB
SPOS = {j: i + 1 for i, j in enumerate((3, 1, 2, 0, 4))}
PRESUM = (1, 2, 0, 4)
W2SRC = (5, 6, 0, 11, 0)
W2COUNT = (2, 4, 6, 8, 9)
SMALL = 10
XDMA, ZDMA = RB, 6


def table_constants():
    kr = np.arange(P)[:, None] // C
    e = np.arange(NE)[None, :]
    yy = (RB * (e // RB) - e % RB + kr - PAD1).astype(np.float32)
    mask = np.where(np.abs(yy) <= PAD1, 0.0, -1e30).astype(np.float32)
    grp = (np.arange(P) % C) // (C // GROUPS)
    gm = (grp[:, None] == grp[None, :]).astype(np.float32) / np.float32(N_GROUP)
    return np.concatenate([yy, yy * yy, mask, gm], axis=1).astype(np.float32)


def build(nc, x, w0, bias, w1, tables, out):
    with ExitStack() as ctx:
        def sb(name, shape, dt=F32):
            return ctx.enter_context(nc.sbuf_tensor(name, shape, dt))

        def sem(name):
            return ctx.enter_context(nc.semaphore(name))

        X = sb("X", [P, NP * PAIR])
        P1 = sb("P1", [P, R1, W1])
        Z = sb("Z", [P, R2, W])
        P2 = sb("P2", [P, R2, W2])
        pre = {1: sb("pre1", [P, 4, R1 * U1]), 2: sb("pre2", [P, 4, R2 * U2])}
        s32 = {1: sb("s32_1", [P, 5, R1 * U1]), 2: sb("s32_2", [P, 5, R2 * U2])}
        hi = {1: sb("hi1", [P, 5, R1, U1], F16), 2: sb("hi2", [P, 5, R2, U2], F16)}
        lo = {1: sb("lo1", [P, 5, R1, U1], F16), 2: sb("lo2", [P, 5, R2, U2], F16)}
        wh = {1: sb("wh1", [P, 5, G1 * KB1 * P], F16), 2: sb("wh2", [P, 5, G2 * KB2 * P], F16)}
        wl = {1: sb("wl1", [P, 5, G1 * KB1 * P], F16), 2: sb("wl2", [P, 5, G2 * KB2 * P], F16)}
        m1b = {1: sb("m1b1", [P, OUTN]), 2: sb("m1b2", [P, OUTN])}
        psum_ = {1: sb("ps1", [P, OUTN]), 2: sb("ps2", [P, OUTN])}
        pdif = {1: sb("pd1", [P, OUTN]), 2: sb("pd2", [P, OUTN])}
        osc = {1: sb("osc1", [P, 4]), 2: sb("osc2", [P, 4])}
        bias_c = {1: sb("bias1", [P, 1]), 2: sb("bias2", [P, 1])}
        warm = sb("warm", [P, 1])
        junk = sb("junk", [P, 2, T * W], BF16)
        sums = {1: sb("sums1", [P, 4]), 2: sb("sums2", [P, 4])}
        mom = {1: sb("mom1", [P, 2, IMG]), 2: sb("mom2", [P, 2, IMG])}
        msq = {1: sb("msq1", [P, IMG]), 2: sb("msq2", [P, IMG])}
        var = {1: sb("var1", [P, IMG]), 2: sb("var2", [P, IMG])}
        vare = {1: sb("vare1", [P, IMG]), 2: sb("vare2", [P, IMG])}
        std = {1: sb("std1", [P, IMG]), 2: sb("std2", [P, IMG])}
        rcp = {1: sb("rcp1", [P, IMG]), 2: sb("rcp2", [P, IMG])}
        gsc = {1: sb("gsc1", [P, IMG]), 2: sb("gsc2", [P, IMG])}
        gof = {1: sb("gof1", [P, IMG]), 2: sb("gof2", [P, IMG])}
        tab = sb("tab", [P, 3 * NE + P])
        yy_t, yy2_t, mask_t = (tab[:, i * NE:(i + 1) * NE] for i in range(3))
        group_t = tab[:, 3 * NE:3 * NE + P]
        prm = sb("prm", [P, C, 3])
        turn = sb("turn", [P, 2, C])
        rnd = sb("rnd", [P, 2, C])
        rnd2 = sb("rnd2", [P, 2, C])
        frac = sb("frac", [P, 2, C])
        sc = sb("sc", [P, 2, C])
        scq = sb("scq", [P, 2, C])
        wq = sb("wq", [P, 2, C])
        q = sb("q", [P, 16, C])
        bt = sb("bt", [P, NE, C])
        ca = pre[2][:, :, 0:NE * C]
        ak = sb("ak", [P, 4, C])
        arg = sb("arg", [P, K1, NE * C])
        ker = arg
        gt = sb("gt", [P, 5, G1 * NE * C])
        ksg = sb("ksg", [P, G1, C])
        ksum = sb("ksum", [P, C])
        krec = sb("krec", [P, C])
        rs = sb("rs", [P, 5, C])
        NW2 = KB2 * RB
        stage = sb("stage", [P, C, NW2 * K2])
        g2t = sb("g2t", [P, 8, NW2, C])
        wmax = sb("wmax", [P, 1])
        wall = sb("wall", [P, 1])
        wclamp = sb("wclamp", [P, 1])
        wpow = sb("wpow", [P, 1], I32)
        winv = sb("winv", [P, 1], I32)
        wsj = sb("wsj", [P, 4])

        banks = ctx.enter_context(nc.psum_tensor("banks", [P, 8, 512], F32))
        BANK = {1: (0, 1, 2, 3, 4), 2: (5, 6, 0, 1, 2)}
        STAT = {1: banks[:, 7, 0:4], 2: banks[:, 7, 4:8]}

        x_loaded = sem("x_loaded")
        tab_loaded = sem("tab_loaded")
        prm_loaded = sem("prm_loaded")
        bias_loaded = sem("bias_loaded")
        stage_loaded = sem("stage_loaded")
        z_loaded = sem("z_loaded")
        stored = sem("stored")
        pads_zero = sem("pads_zero")
        stage_zero = sem("stage_zero")
        consts_set = sem("consts_set")
        sums_done = {1: sem("sums1_done"), 2: sem("sums2_done")}
        stat_mm = {1: sem("stat1_mm"), 2: sem("stat2_mm")}
        small = {1: sem("small1"), 2: sem("small2")}
        std_done = {1: sem("std1_done"), 2: sem("std2_done")}
        norm_done = {1: sem("norm1_done"), 2: sem("norm2_done")}
        pre_done = {1: sem("pre1_done"), 2: sem("pre2_done")}
        s_done = {1: sem("s1_done"), 2: sem("s2_done")}
        hi_done = {1: sem("hi1_done"), 2: sem("hi2_done")}
        lo_done = {1: sem("lo1_done"), 2: sem("lo2_done")}
        conv_mm = {1: sem("conv1_mm"), 2: sem("conv2_mm")}
        m1_read = {1: sem("m1_read1"), 2: sem("m1_read2")}
        mid_done = {1: sem("mid1_done"), 2: sem("mid2_done")}
        res_done = {1: sem("res1_done"), 2: sem("res2_done")}
        out_done = {1: sem("out1_done"), 2: sem("out2_done")}
        dve_w = sem("dve_w")
        pool_w = sem("pool_w")
        sin_done = sem("sin_done")
        exp_done = sem("exp_done")
        wh1_done = sem("wh1_done")
        wl1_done = sem("wl1_done")
        wh2_done = sem("wh2_done")
        wl2_done = sem("wl2_done")
        wmax_done = sem("wmax_done")

        def pair(n):
            return X[:, bass.ds(n * PAIR, PAIR)]

        def image(n, i):
            return pair(n).rearrange("p (t m x) -> p t m x", t=T, m=IMG)[:, :, i, :]

        def cols(n, v):
            return pair(n).rearrange("p (r u v) -> p (r u) v", u=U, v=3)[:, :, v]

        USED = {1: {0: (1, U1), 1: (1, U1 - 1), 2: (1, U1 - 1), 3: (0, U1), 4: (0, U1 - 1)},
                2: {0: (0, U2), 1: (0, U2), 2: (0, U2), 3: (0, U2), 4: (0, U2 - 1)}}
        NU = {1: U1, 2: U2}

        def dcol(c, k, j):
            lo_, hi_ = USED[c][j]
            return (P1 if c == 1 else P2)[:, :, 3 * lo_ + k:3 * (hi_ - 1) + k + 1:3]

        def tiles(buf, c, i, j):
            lo_, hi_ = USED[c][j]
            return buf[c][:, i, :].rearrange("p (r u) -> p r u", u=NU[c])[:, :, lo_:hi_]

        def half(buf, c, j):
            lo_, hi_ = USED[c][j]
            if j == 3 and c == 1:
                lo_, hi_ = 1, U1 - 1
            return buf[c][:, j, :, lo_:hi_]

        def full(c, j):
            if j == 3 and c == 1:
                return tiles(s32, 1, 3, 1)
            return tiles(s32, c, j, j)

        def tap2(k):
            return stage[:, :, :].rearrange("p o (e j) -> p e o j", j=K2)[:, :, :, K2 - 1 - k]

        def W2PARTS(j):
            return {0: ((0, tap2(0), 1), (1, tap2(3), 1)),
                    1: ((0, g2t[:, 1, :, :], 2), (1, g2t[:, 2, :, :], 2)),
                    2: ((0, g2t[:, 3, :, :], 3), (1, g2t[:, 4, :, :], 3)),
                    3: ((0, g2t[:, 7, :, :], 3), (1, g2t[:, 6, :, :], 3)),
                    4: ((0, tap2(2), 0),)}[j]

        block = ctx.enter_context(nc.Block())

        def wait(eng, s, v):
            if isinstance(v, int) and v <= 0:
                return
            eng.wait_ge(s, v)

        MARK = {}

        def pre_sum(nce, eng, c, n, i):
            j = PRESUM[i]
            a, b, op = ((1, 2, ALU.add), (1, 2, ALU.subtract), (0, 2, ALU.subtract), (4, 2, ALU.subtract))[i]
            if i == 0:
                eng.wait_ge(norm_done[c], IMG * (n + 1))
                wait(eng, s_done[c], 5 * n)
            nce.tensor_tensor(tiles(pre, c, i, j), dcol(c, a, j), dcol(c, b, j), op).then_inc(pre_done[c], 1)

        def addressed(eng):
            eng.nop(nofuse=True)
            eng.wait_ge(consts_set, 1)

        @block.sync
        def _(sp):
            def rows(dram, n):
                return dram[bass.ds(n * IMG, IMG)].rearrange("m c (t k) x -> k c t m x", k=RB)

            def load(n):
                for k in range(RB):
                    dst = pair(n)[k * C:(k + 1) * C].rearrange("p (t m x) -> p t m x", t=T, m=IMG)
                    sp.dma_start(dst, rows(x, n)[k]).then_inc(x_loaded, 16)

            def store(n):
                sp.wait_ge(out_done[2], 5 * n + 5)
                for k in range(RB):
                    src = pair(n)[k * C:(k + 1) * C].rearrange("p (t m x) -> p t m x", t=T, m=IMG)
                    sp.dma_start(rows(out, n)[k], src).then_inc(stored, 16)

            def shift(n):
                RW = IMG * W
                zf = Z[:, :, :].rearrange("p r x -> p (r x)")
                src = pair(n)
                sp.wait_ge(out_done[1], 5 * n + 5)
                wait(sp, norm_done[2], n)
                sp.dma_start(zf[C:P, 0:PAIR], src[0:P - C, :]).then_inc(z_loaded, 16)
                sp.dma_start(zf[0:C, RW:RW + PAIR], src[P - C:P, :]).then_inc(z_loaded, 16)
                ends = ((0, 0, 1), (1, T, H - 2), (2, T, H - 3), (3, T, 2))
                for k, t, r in ends:
                    kr, tr = r % RB, r // RB
                    sp.dma_start(zf[k * C:(k + 1) * C, t * RW:(t + 1) * RW],
                                 src[kr * C:(kr + 1) * C, tr * RW:(tr + 1) * RW]).then_inc(z_loaded, 16)

            PER = XDMA * 16
            for k in range(2):
                sp.dma_start(prm[k * C:(k + 1) * C], w0.rearrange("o c j -> c o j")).then_inc(prm_loaded, 16)
            load(0)
            sp.wait_ge(stage_zero, 1)
            for k in range(RB):
                sp.dma_start(stage[k * C:(k + 1) * C, :, k * K2:k * K2 + K2 * K2],
                             w1.rearrange("o c i j -> c o (i j)")).then_inc(stage_loaded, 16)
            for k in range(RB):
                sp.dma_start(bias_c[1][k * C:(k + 1) * C, :], bias.rearrange("(o i) -> o i", i=1)).then_inc(bias_loaded, 16)
            sp.wait_ge(x_loaded, PER)
            load(1)
            sp.wait_ge(x_loaded, 2 * PER)
            load(2)

            def step(n, prefetch, last=False):
                if prefetch:
                    sp.wait_ge(x_loaded, PER * (n + 3))
                    load(n + 3)
                if not last:
                    shift(n)
                if not (isinstance(n, int) and n == 0):
                    store(n - 1)

            step(0, True)
            step(1, True)
            with sp.Fori(2, NP - 3) as n:
                step(n, True)
            step(NP - 3, False)
            step(NP - 2, False)
            step(NP - 1, False)
            step(NP, False, last=True)
            sp.wait_ge(stored, 16 * RB * NP)

        @block.vector
        def _(dve):
            count = [0]

            def done(ins):
                count[0] += 1
                ins.then_inc(dve_w, 1)

            def stage_end():
                dve.wait_ge(dve_w, count[0])

            tt, ts, stt = nc.vector.tensor_tensor, nc.vector.tensor_scalar, nc.vector.scalar_tensor_tensor

            def angles():
                dve.wait_ge(prm_loaded, 16 * RB)
                done(ts(turn[:, 0, :], prm[:, :, 2], 1.0 / 360.0, None, ALU.mult))
                done(ts(turn[:, 1, :], prm[:, :, 2], 1.0 / 360.0, 0.25, ALU.mult, ALU.add))
                stage_end()
                done(ts(rnd[:, :, :], turn[:, :, :], ROUND, None, ALU.add))
                stage_end()
                done(ts(rnd2[:, :, :], rnd[:, :, :], -ROUND, None, ALU.add))
                stage_end()
                done(tt(frac[:, :, :], turn[:, :, :], rnd2[:, :, :], ALU.subtract))
                MARK["angle"] = count[0]

            def covariance():
                mul = ALU.mult
                done(tt(wq[:, 0, :], prm[:, :, 0], prm[:, :, 0], mul))
                done(tt(wq[:, 1, :], prm[:, :, 1], prm[:, :, 1], mul))
                dve.wait_ge(sin_done, 1)
                done(tt(scq[:, :, :], sc[:, :, :], sc[:, :, :], mul))
                done(tt(q[:, 0, :], sc[:, 0, :], sc[:, 1, :], mul))
                stage_end()
                done(tt(q[:, 1, :], scq[:, 1, :], wq[:, 0, :], mul))
                done(tt(q[:, 2, :], scq[:, 0, :], wq[:, 1, :], mul))
                done(tt(q[:, 3, :], scq[:, 0, :], wq[:, 0, :], mul))
                done(tt(q[:, 4, :], scq[:, 1, :], wq[:, 1, :], mul))
                done(tt(q[:, 5, :], wq[:, 0, :], wq[:, 1, :], ALU.subtract))
                stage_end()
                done(tt(q[:, 6, :], q[:, 1, :], q[:, 2, :], ALU.add))
                done(tt(q[:, 7, :], q[:, 3, :], q[:, 4, :], ALU.add))
                done(tt(q[:, 8, :], q[:, 0, :], q[:, 5, :], mul))
                stage_end()
                done(tt(q[:, 9, :], q[:, 6, :], q[:, 7, :], mul))
                done(tt(q[:, 10, :], q[:, 8, :], q[:, 8, :], mul))
                stage_end()
                done(tt(q[:, 11, :], q[:, 9, :], q[:, 10, :], ALU.subtract))
                stage_end()
                done(nc.vector.reciprocal(q[:, 12, :], q[:, 11, :]))
                stage_end()
                done(stt(q[:, 13, :], q[:, 7, :], -0.5, q[:, 12, :], mul, mul))
                done(tt(q[:, 14, :], q[:, 8, :], q[:, 12, :], mul))
                done(stt(q[:, 15, :], q[:, 6, :], -0.5, q[:, 12, :], mul, mul))
                stage_end()

            def exponents():
                mul = ALU.mult
                dve.wait_ge(tab_loaded, 16)

                def rows(v):
                    return v.unsqueeze(2).to_broadcast([P, NE, C])

                def chans(v):
                    return v.unsqueeze(1).to_broadcast([P, NE, C])

                cc = arg[:, PAD1, :].rearrange("p (e o) -> p e o", o=C)
                done(tt(cc, rows(yy2_t), chans(q[:, 15, :]), mul))
                done(tt(bt[:, :, :], rows(yy_t), chans(q[:, 14, :]), mul))
                for k in range(1, 5):
                    done(ts(ak[:, k - 1, :], q[:, 13, :], float(k * k), None, mul))
                stage_end()
                done(tt(cc, cc, rows(mask_t), ALU.add))
                stage_end()
                for k in range(1, 5):
                    done(tt(ca[:, k - 1, :].rearrange("p (e o) -> p e o", o=C), cc, chans(ak[:, k - 1, :]), ALU.add))
                stage_end()
                btf = bt[:, :, :].rearrange("p e o -> p (e o)")
                taps = iter(range(K1))

                def next_exponent():
                    t = next(taps, None)
                    if t == PAD1:
                        t = next(taps)
                    if t is not None:
                        k = t - PAD1
                        done(stt(arg[:, t, :], btf, float(k), ca[:, abs(k) - 1, :], mul, ALU.add))
                        if t % 3 == 2:
                            MARK["exponents", t // 3] = count[0]

                small_stats(1, 0, fill=next_exponent)
                for _ in range(K1):
                    next_exponent()

            def tap(k):
                return ker[:, :, :].rearrange("p (g k) e -> p g k e", k=3)[:, :, k, :]

            def gtv(i):
                return gt[:, i, :].rearrange("p (g e) -> p g e", g=G1)

            def kernel_sums():
                for g in range(G1):
                    dve.wait_ge(exp_done, g + 1)
                    done(tt(gtv(0)[:, g], tap(0)[:, g], tap(2)[:, g], ALU.add))
                    stage_end()
                    done(tt(gtv(1)[:, g], gtv(0)[:, g], tap(1)[:, g], ALU.add))
                    stage_end()
                    done(nc.vector.tensor_reduce(ksg[:, g, :], gtv(1)[:, g].rearrange("p (r o) -> p o r", o=C), AX_X, ALU.add))
                stage_end()
                done(tt(ksg[:, 0, :], ksg[:, 0, :], ksg[:, 1, :], ALU.add))
                stage_end()
                done(tt(ksum[:, :], ksg[:, 0, :], ksg[:, 2, :], ALU.add))
                stage_end()
                done(nc.vector.reciprocal(krec[:, :], ksum[:, :]))
                stage_end()
                for j in STREAMS:
                    done(ts(rs[:, j, :], krec[:, :], W1_SCALE * G_FACTOR[j], None, ALU.mult))
                stage_end()

            def kernel_stream(k):
                mul = ALU.mult
                j = STREAMS[k]
                if j == 2:
                    done(tt(gtv(2), tap(1), gtv(0), ALU.subtract))
                    stage_end()
                if j == 3:
                    done(stt(gtv(4), tap(1), 2.0, tap(0), mul, ALU.add))
                    stage_end()
                    done(stt(gtv(3), tap(2), 4.0, gtv(4), mul, ALU.add))
                    stage_end()
                src = {0: tap(0), 4: tap(2)}.get(j)
                if src is None:
                    done(tt(gt[:, j, :].rearrange("p (r o) -> p r o", o=C),
                            gt[:, j, :].rearrange("p (r o) -> p r o", o=C),
                            rs[:, j, :].unsqueeze(1).to_broadcast([P, G1 * NE, C]), mul))
                else:
                    for g in range(G1):
                        done(tt(gt[:, j, g * NE * C:(g + 1) * NE * C].rearrange("p (e o) -> p e o", o=C),
                                src[:, g, :].rearrange("p (e o) -> p e o", o=C),
                                rs[:, j, :].unsqueeze(1).to_broadcast([P, NE, C]), mul))
                MARK["scaled", k] = count[0]

            def layer2_largest():
                dve.wait_ge(stage_loaded, 16 * RB)
                done(nc.vector.tensor_reduce(wmax[:, :], stage[:, :, :].rearrange("p o e -> p (o e)"), AX_X, ALU.max,
                                             apply_absolute_value=True))
                MARK["largest2"] = count[0]

            def layer2_scale():
                dve.wait_ge(wmax_done, 1)
                done(ts(wclamp[:, :], wall[:, :], 1e-30, None, ALU.max))
                stage_end()
                done(ts(wpow[:, :], wclamp[:, :].bitcast(I32), 0x7F800000, None, ALU.bitwise_and))
                stage_end()
                done(ts(winv[:, :], wpow[:, :], -1.0, float(0x7F000000), ALU.mult, ALU.add))
                for f, v in enumerate((1.0, -1.0, 2.0, 4.0)):
                    done(ts(osc[2][:, f:f + 1], wpow[:, :].bitcast(F32), v / (X_SCALE * W2_SCALE), None, ALU.mult))
                stage_end()
                for f, v in enumerate((1.0, 0.5, -0.5, 1 / 6)):
                    done(ts(wsj[:, f:f + 1], winv[:, :].bitcast(F32), v * W2_SCALE, None, ALU.mult))
                stage_end()
                MARK["scale2"] = count[0]

            def low_layer2():
                m = 0
                for k in range(5):
                    j = STREAMS[k]
                    dve.wait_ge(pool_w, W2SRC[k])
                    for g, src, f in W2PARTS(j):
                        m += 1
                        dve.wait_ge(wh2_done, m)
                        sl = slice(g * NW2 * C, (g + 1) * NW2 * C)
                        stt(wl[2][:, j, sl].rearrange("p (e o) -> p e o", o=C), src, wsj[:, f:f + 1],
                            wh[2][:, j, sl].rearrange("p (e o) -> p e o", o=C), ALU.mult, ALU.subtract).then_inc(wl2_done, 1)

            def small_stats(c, n, fill=lambda: None):
                dve.wait_ge(stat_mm[c], n + 1)
                wait(dve, norm_done[c], IMG * n)
                nc.vector.tensor_copy(mom[c][:, :, :].rearrange("p a b -> p (a b)"), STAT[c]).then_inc(small[c], 1)
                mean, ex2 = mom[c][:, 0, :], mom[c][:, 1, :]
                at = SMALL * n
                fill()
                dve.wait_ge(small[c], at + 1)
                stt(msq[c][:, :], mean, -1.0, mean, ALU.mult, ALU.mult).then_inc(small[c], 1)
                fill()
                dve.wait_ge(small[c], at + 2)
                tt(var[c][:, :], ex2, msq[c][:, :], ALU.add).then_inc(small[c], 1)
                fill()
                dve.wait_ge(small[c], at + 3)
                ts(vare[c][:, :], var[c][:, :], 0.0, EPS, ALU.max, ALU.add).then_inc(small[c], 1)
                fill()
                fill()
                dve.wait_ge(std_done[c], n + 1)
                nc.vector.reciprocal(rcp[c][:, :], std[c][:, :]).then_inc(small[c], 1)
                fill()
                dve.wait_ge(small[c], at + 5)
                stt(msq[c][:, :], vare[c][:, :], 1.0 / (X_SCALE * X_SCALE), rcp[c][:, :], ALU.mult, ALU.mult).then_inc(small[c], 1)
                fill()
                dve.wait_ge(small[c], at + 6)
                tt(var[c][:, :], msq[c][:, :], rcp[c][:, :], ALU.mult).then_inc(small[c], 1)
                fill()
                dve.wait_ge(small[c], at + 7)
                ts(msq[c][:, :], var[c][:, :], -0.5, 1.5, ALU.mult, ALU.add).then_inc(small[c], 1)
                fill()
                dve.wait_ge(small[c], at + 8)
                tt(gsc[c][:, :], msq[c][:, :], rcp[c][:, :], ALU.mult).then_inc(small[c], 1)
                fill()
                dve.wait_ge(small[c], at + 9)
                stt(gof[c][:, :], mean, -1.0, gsc[c][:, :], ALU.mult, ALU.mult).then_inc(small[c], 1)

            def stream3(c, n):
                dve.wait_ge(norm_done[c], IMG * (n + 1))
                wait(dve, lo_done[c], 5 * n)
                tt(tiles(s32, c, 3, 3), dcol(c, 3, 3), dcol(c, 1, 3), ALU.subtract).then_inc(s_done[c], 1)

            def make_stream(c, n, i):
                j = PRESUM[i]
                dve.wait_ge(pre_done[c], 4 * n + i + 1)
                if i == 0:
                    dve.wait_ge(s_done[c], 5 * n + 1)
                a, t_, dst = tiles(s32, c, 3, j), tiles(pre, c, i, j), tiles(s32, c, j, j)
                if j == 1:
                    tt(dst, a, t_, ALU.subtract).then_inc(s_done[c], 1)
                elif j == 2:
                    stt(dst, t_, 3.0, a, ALU.mult, ALU.add).then_inc(s_done[c], 1)
                elif j == 0:
                    stt(dst, t_, 2.0, a, ALU.mult, ALU.add).then_inc(s_done[c], 1)
                else:
                    stt(dst, a, -2.0, t_, ALU.mult, ALU.add).then_inc(s_done[c], 1)

            def low_half(c, n, k):
                j = STREAMS[k]
                dve.wait_ge(hi_done[c], 5 * n + k + 1)
                tt(half(lo, c, j), full(c, j), half(hi, c, j), ALU.subtract).then_inc(lo_done[c], 1)

            def own_stream(c, n, i):
                pre_sum(nc.vector, dve, c, n, i)
                make_stream(c, n, i)

            def product(c, k):
                return banks[:, BANK[c][k], 0:OUTN]

            def middle(c, n):
                dve.wait_ge(conv_mm[c], 5 * n + 2)
                dve.wait_ge(m1_read[c], n + 1)
                wait(dve, res_done[c], 3 * n)
                stt(psum_[c][:, :], product(c, 1), osc[c][:, 0:1], m1b[c][:, :], ALU.mult, ALU.add).then_inc(mid_done[c], 1)
                stt(pdif[c][:, :], product(c, 1), osc[c][:, 1:2], m1b[c][:, :], ALU.mult, ALU.add).then_inc(mid_done[c], 1)

            def add_m0(c, n):
                dve.wait_ge(conv_mm[c], 5 * n + 3)
                dve.wait_ge(res_done[c], 3 * n + 1)
                stt(cols(n, 0), product(c, 2), osc[c][:, 0:1], cols(n, 0), ALU.mult, ALU.add).then_inc(out_done[c], 1)

            def add_m3(c, n):
                dve.wait_ge(conv_mm[c], 5 * n + 4)
                dve.wait_ge(res_done[c], 3 * n + 3)
                stt(cols(n, 1), product(c, 3), osc[c][:, 2:3], cols(n, 1), ALU.mult, ALU.add).then_inc(out_done[c], 1)
                stt(cols(n, 2), product(c, 3), osc[c][:, 3:4], cols(n, 2), ALU.mult, ALU.add).then_inc(out_done[c], 1)
                dve.wait_ge(out_done[c], 5 * n + 1)
                stt(cols(n, 0), product(c, 3), osc[c][:, 0:1], cols(n, 0), ALU.mult, ALU.add).then_inc(out_done[c], 1)

            def add_m4(c, n):
                dve.wait_ge(conv_mm[c], 5 * n + 5)
                dve.wait_ge(out_done[c], 5 * n + 3)
                stt(cols(n, 2), product(c, 4), osc[c][:, 0:1], cols(n, 2), ALU.mult, ALU.add).then_inc(out_done[c], 1)

            angles()
            covariance()
            exponents()
            stream3(1, 0)
            own_stream(1, 0, 0)
            kernel_sums()
            kernel_stream(0)
            low_half(1, 0, 0)
            kernel_stream(1)
            own_stream(1, 0, 1)
            own_stream(1, 0, 2)
            low_half(1, 0, 1)
            kernel_stream(2)
            low_half(1, 0, 2)
            kernel_stream(3)
            low_half(1, 0, 3)
            own_stream(1, 0, 3)
            kernel_stream(4)
            low_half(1, 0, 4)
            layer2_largest()
            dve.wait_ge(consts_set, 1)

            def streams_ahead(c, n):
                stream3(c, n)
                make_stream(c, n, 0)
                make_stream(c, n, 1)
                low_half(c, n, 0)
                make_stream(c, n, 2)
                low_half(c, n, 1)
                make_stream(c, n, 3)

            def step(n, prep, ahead, first=False, last=False):
                if first:
                    small_stats(1, 1)
                if last:
                    stream3(2, n - 1)
                    own_stream(2, n - 1, 0)
                    own_stream(2, n - 1, 1)
                    low_half(2, n - 1, 0)
                    own_stream(2, n - 1, 2)
                    low_half(2, n - 1, 1)
                    own_stream(2, n - 1, 3)
                elif not first:
                    streams_ahead(2, n - 1)
                if not first:
                    for k in range(2, 5):
                        low_half(2, n - 1, k)
                if last:
                    add_m3(2, n - 2)
                    add_m4(2, n - 2)
                if not last:
                    middle(1, n)
                if prep:
                    streams_ahead(1, n + 1)
                if not last:
                    add_m0(1, n)
                if prep:
                    low_half(1, n + 1, 2)
                if not last:
                    add_m3(1, n)
                if prep:
                    low_half(1, n + 1, 3)
                if ahead:
                    small_stats(1, n + 2)
                if not last:
                    add_m4(1, n)
                if prep:
                    low_half(1, n + 1, 4)
                if first:
                    layer2_scale()
                    low_layer2()
                if not last and not prep:
                    small_stats(2, n)
                if not first:
                    middle(2, n - 1)
                    add_m0(2, n - 1)
                if prep:
                    small_stats(2, n)
                if not first and (prep or last):
                    add_m3(2, n - 1)
                    add_m4(2, n - 1)

            step(0, True, True, first=True)
            step(1, True, True)
            with dve.Fori(2, NP - 2) as n:
                step(n, True, True)
            step(NP - 2, True, False)
            step(NP - 1, False, False)
            step(NP, False, False, last=True)

        @block.scalar
        def _(act):
            for k in range(2, RB):
                act.dma_start(prm[k * C:(k + 1) * C], w0.rearrange("o c j -> c o j")).then_inc(prm_loaded, 16)
            act.dma_start(tab[:, :], tables).then_inc(tab_loaded, 16)

            def channel_sums(c, n):
                if c == 1:
                    act.wait_ge(x_loaded, 16 * XDMA * (n + 1))
                else:
                    act.wait_ge(out_done[1], 5 * n + 5)
                wait(act, stat_mm[c], n)
                waste = junk[:, c - 1, :].rearrange("p (t x) -> p t x", t=T)
                for i in range(2 * IMG):
                    if i == 0:
                        wait(act, sums_done[c], 2 * IMG * n)
                        addressed(act)
                    else:
                        act.wait_ge(sums_done[c], 2 * IMG * n + i)
                        addressed(act)
                    nc.scalar.activation(waste, image(n, i % IMG), (ACT.Identity, ACT.Square)[i // IMG],
                                         accum_out=sums[c][:, i:i + 1]).then_inc(sums_done[c], 1)

            def standard_deviation(c, n):
                act.wait_ge(small[c], SMALL * n + 4)
                nc.scalar.activation(std[c][:, :], vare[c][:, :], ACT.Sqrt,
                                     scale=1.0 / (X_SCALE * X_SCALE)).then_inc(std_done[c], 1)

            def normalise1(n):
                act.wait_ge(small[1], SMALL * (n + 1))
                wait(act, s_done[1], 5 * n)
                wait(act, pre_done[1], 4 * n)
                act.wait_ge(pads_zero, 1)
                addressed(act)
                for i in range(IMG):
                    dst = P1[:, :, :].rearrange("p (t m) x -> p t m x", m=IMG)[:, :, i, PAD1:PAD1 + W]
                    nc.scalar.activation(dst, image(n, i), ACT.Identity, bias=gof[1][:, i:i + 1],
                                         scale=gsc[1][:, i:i + 1]).then_inc(norm_done[1], 1)

            def normalise2(n):
                act.wait_ge(small[2], SMALL * (n + 1))
                act.wait_ge(z_loaded, ZDMA * 16 * (n + 1))
                wait(act, s_done[2], 5 * n)
                wait(act, pre_done[2], 4 * n)
                for i in range(IMG):
                    src = Z[:, :, :].rearrange("p (t m) x -> p t m x", m=IMG)[:, :, i, :]
                    dst = P2[:, :, :].rearrange("p (t m) x -> p t m x", m=IMG)[:, :, i, :]
                    for d0, d1, ds_, s0, s1, ss in ((1, 1 + W, 1, 0, W, 1), (0, W2, W2 - 1, 1, 3, 1),
                                                    (W + 1, W + 3, 1, W - 2, W - 4, -1)):
                        ins = nc.scalar.activation(dst[:, :, d0:d1:ds_], src[:, :, s0:s1:ss], ACT.Identity,
                                                   bias=gof[2][:, i:i + 1], scale=gsc[2][:, i:i + 1])
                    ins.then_inc(norm_done[2], 1)

            def high_half(c, n, k):
                j = STREAMS[k]
                act.wait_ge(s_done[c], 5 * n + SPOS[j])
                wait(act, conv_mm[c], 5 * n + k + 1 - 5)
                nc.scalar.copy(half(hi, c, j), full(c, j)).then_inc(hi_done[c], 1)

            def read_m1(c, n):
                act.wait_ge(conv_mm[c], 5 * n + 1)
                wait(act, mid_done[c], 2 * n)
                nc.scalar.activation(m1b[c][:, :], banks[:, BANK[c][0], 0:OUTN], ACT.Identity,
                                     bias=bias_c[c][:, 0:1], scale=osc[c][:, 0:1]).then_inc(m1_read[c], 1)

            def high_kernel(k):
                j = STREAMS[k]
                act.wait_ge(dve_w, MARK["scaled", k])
                nc.scalar.copy(wh[1][:, j, :], gt[:, j, :]).then_inc(wh1_done, 1)

            def high_layer2():
                for k in range(5):
                    j = STREAMS[k]
                    act.wait_ge(pool_w, W2SRC[k])
                    act.wait_ge(dve_w, MARK["scale2"])
                    for g, src, f in W2PARTS(j):
                        ins = nc.scalar.mul(wh[2][:, j, g * NW2 * C:(g + 1) * NW2 * C].rearrange("p (e o) -> p e o", o=C),
                                            src, wsj[:, f:f + 1])
                        ins.then_inc(wh2_done, 1)

            act.wait_ge(dve_w, MARK["angle"])
            nc.scalar.activation(sc[:, :, :], frac[:, :, :], ACT.Sin, scale=TWO_PI).then_inc(sin_done, 1)
            channel_sums(1, 0)
            standard_deviation(1, 0)
            act.wait_ge(consts_set, 1)
            nc.scalar.activation(warm[:, :], bias_c[2][:, :], ACT.Exp)
            normalise1(0)
            for g in range(3):
                act.wait_ge(dve_w, MARK["exponents", g])
                nc.scalar.activation(ker[:, 3 * g:3 * g + 3, :], arg[:, 3 * g:3 * g + 3, :], ACT.Exp).then_inc(exp_done, 1)
            high_half(1, 0, 0)
            channel_sums(1, 1)
            high_kernel(0)
            high_kernel(1)
            high_half(1, 0, 1)
            high_half(1, 0, 2)
            high_kernel(2)
            high_half(1, 0, 3)
            high_kernel(3)
            high_half(1, 0, 4)
            high_kernel(4)
            act.wait_ge(bias_loaded, 16 * RB)

            def step(n, prep, ahead, first=False, last=False):
                if first:
                    standard_deviation(1, 1)
                if not first:
                    normalise2(n - 1)
                if prep:
                    normalise1(n + 1)
                if not first:
                    high_half(2, n - 1, 0)
                    high_half(2, n - 1, 1)
                if not last:
                    read_m1(1, n)
                if not first:
                    for k in range(2, 5):
                        high_half(2, n - 1, k)
                if ahead:
                    channel_sums(1, n + 2)
                if prep:
                    for k in range(4):
                        high_half(1, n + 1, k)
                if ahead:
                    standard_deviation(1, n + 2)
                if prep:
                    high_half(1, n + 1, 4)
                if not last:
                    channel_sums(2, n)
                if not last and not prep:
                    standard_deviation(2, n)
                if first:
                    high_layer2()
                if not first:
                    read_m1(2, n - 1)
                if prep:
                    standard_deviation(2, n)

            step(0, True, True, first=True)
            step(1, True, True)
            with act.Fori(2, NP - 2) as n:
                step(n, True, True)
            step(NP - 2, True, False)
            step(NP - 1, False, False)
            step(NP, False, False, last=True)

        @block.gpsimd
        def _(pool):
            nc.gpsimd.memset(stage[:, :, :], 0.0).then_inc(stage_zero, 1)
            nc.gpsimd.memset(P1[:, :, :], 0.0).then_inc(pads_zero, 1)
            for f, v in enumerate((1.0, -1.0, 2.0, 4.0)):
                nc.gpsimd.memset(osc[1][:, f:f + 1], v / (X_SCALE * W1_SCALE))
            nc.gpsimd.memset(bias_c[2][:, :], 0.0).then_inc(consts_set, 1)

            tt, ts = nc.gpsimd.tensor_tensor, nc.gpsimd.tensor_scalar
            count = [0]

            def done(ins):
                count[0] += 1
                ins.then_inc(pool_w, 1)

            def stage_end():
                pool.wait_ge(pool_w, count[0])

            def layer2_taps():
                marks = [0] * 5
                done(tt(g2t[:, 0, :, :], tap2(0), tap2(2), ALU.add))
                done(tt(g2t[:, 2, :, :], tap2(3), tap2(4), ALU.add))
                done(tt(g2t[:, 4, :, :], tap2(4), tap2(3), ALU.subtract))
                done(ts(g2t[:, 7, :, :], tap2(1), 2.0, None, ALU.mult))
                stage_end()
                done(tt(g2t[:, 1, :, :], g2t[:, 0, :, :], tap2(1), ALU.add))
                done(tt(g2t[:, 3, :, :], tap2(1), g2t[:, 0, :, :], ALU.subtract))
                stage_end()
                done(tt(g2t[:, 5, :, :], g2t[:, 7, :, :], tap2(0), ALU.add))
                done(ts(g2t[:, 0, :, :], tap2(2), 4.0, None, ALU.mult))
                stage_end()
                done(tt(g2t[:, 7, :, :], g2t[:, 5, :, :], g2t[:, 0, :, :], ALU.add))
                stage_end()
                done(ts(g2t[:, 5, :, :], tap2(4), 2.0, None, ALU.mult))
                stage_end()
                done(tt(g2t[:, 6, :, :], g2t[:, 5, :, :], tap2(3), ALU.add))
                assert count[0] == W2SRC[3], count[0]

            def pre_sums(c, n):
                for i in range(4):
                    pre_sum(nc.gpsimd, pool, c, n, i)

            def low_kernel(k):
                j = STREAMS[k]
                pool.wait_ge(wh1_done, k + 1)
                tt(wl[1][:, j, :], gt[:, j, :], wh[1][:, j, :], ALU.subtract).then_inc(wl1_done, 1)

            def residual(c, n):
                for i, (v, src) in enumerate(((0, psum_), (1, pdif), (2, psum_))):
                    if i == 0:
                        pool.wait_ge(mid_done[c], 2 * n + 1)
                        if c == 1:
                            pool.wait_ge(norm_done[1], IMG * (n + 1))
                        else:
                            pool.wait_ge(z_loaded, ZDMA * 16 * (n + 1))
                            pool.wait_ge(sums_done[2], 2 * IMG * (n + 1))
                    if i == 1:
                        pool.wait_ge(mid_done[c], 2 * n + 2)
                    addressed(pool)
                    tt(cols(n, v), cols(n, v), src[c][:, :], ALU.add).then_inc(res_done[c], 1)

            pool.wait_ge(pads_zero, 1)
            for k in range(5):
                low_kernel(k)

            def step(n, prep, first=False, last=False):
                if not first and not last:
                    pre_sums(2, n - 1)
                if prep:
                    pre_sums(1, n + 1)
                if not last:
                    residual(1, n)
                if first:
                    pool.wait_ge(dve_w, MARK["largest2"])
                    nc.gpsimd.partition_all_reduce(wall[:, :], wmax[:, :], P, RMAX).then_inc(wmax_done, 1)
                    layer2_taps()
                if not first:
                    residual(2, n - 1)

            step(0, True, first=True)
            step(1, True)
            with pool.Fori(2, NP - 1) as n:
                step(n, True)
            step(NP - 1, False)
            step(NP, False, last=True)

        @block.tensor
        def _(pe):
            KB = {1: KB1, 2: KB2}
            G = {1: G1, 2: G2}

            def stats(c, n):
                pe.wait_ge(sums_done[c], 2 * IMG * (n + 1))
                nc.tensor.matmul(STAT[c], group_t, sums[c][:, :], start=True, stop=True).then_inc(stat_mm[c], 1)

            def spans(c, j, g, b):
                if c == 2:
                    return (0, R1), (IMG * b, IMG * b + R1), (0, U)
                rows_out = ((IMG, R1), (0, R1), (0, R1 - IMG))[b]
                rows_in = ((0, R1 - IMG), (0, R1), (IMG, R1))[b]
                u0 = 1 if g == 0 and j != 4 else 0
                u1 = U - 1 if g == G1 - 1 and j != 0 else U
                return rows_out, rows_in, (u0, u1)

            def conv_stream(c, n, k, first=False):
                j = STREAMS[k]
                groups = 1 if (c == 2 and j == 4) else G[c]
                steps = [(g, b) for g in range(groups) for b in range(KB[c])]
                steps.sort(key=lambda gb: gb != ((1, 1) if c == 1 else (0, 0)))
                dst = banks[:, BANK[c][k], 0:OUTN].rearrange("p (r u) -> p r u", u=U)
                parts = ((wh, hi), (wh, lo), (wl, hi))
                for part, (wbuf, xbuf) in enumerate(parts):
                    if part == 0:
                        pe.wait_ge(hi_done[c], 5 * n + k + 1)
                        if first:
                            pe.wait_ge(wh1_done, k + 1)
                    if part == 1:
                        pe.wait_ge(lo_done[c], 5 * n + k + 1)
                    if part == 2 and first:
                        pe.wait_ge(wl1_done, k + 1)
                    for i, (g, b) in enumerate(steps):
                        block_at = b if c == 1 else KB2 - 1 - b
                        at = (g * KB[c] + block_at) * P
                        (o0, o1), (i0, i1), (u0, u1) = spans(c, j, g, b)
                        ins = nc.tensor.matmul(dst[:, o0:o1, u0:u1], wbuf[c][:, j, at:at + P],
                                               xbuf[c][:, j, i0:i1, g + u0:g + u1],
                                               start=(part == 0 and i == 0),
                                               stop=(part == 2 and i == len(steps) - 1))
                ins.then_inc(conv_mm[c], 1)

            def bank_free(c, n, k, final=False):
                if c == 1:
                    if k < 3:
                        wait(pe, out_done[2], 5 * (n - 2) + (1, 4, 5)[k])
                        if isinstance(n, int) and n == 1:
                            pe.wait_ge(*((m1_read[1], 1), (mid_done[1], 2), (out_done[1], 1))[k])
                    else:
                        wait(pe, out_done[1], 5 * (n - 1) + (4, 5)[k - 3])
                elif k == 0:
                    wait(pe, m1_read[2], n)
                elif k == 1:
                    wait(pe, mid_done[2], 2 * n)
                elif final:
                    pe.wait_ge(out_done[2], 5 * (n - 1) + (1, 4, 5)[k - 2])
                elif k == 2:
                    pe.wait_ge(m1_read[1], n + 2)
                elif k == 3:
                    pe.wait_ge(mid_done[1], 2 * (n + 2))
                else:
                    pe.wait_ge(out_done[1], 5 * (n + 1) + 1)

            def step(n, prep, ahead, first=False, last=False):
                if not last:
                    for k in range(5):
                        bank_free(1, n, k)
                        conv_stream(1, n, k, first)
                        if k == 0 and isinstance(n, int) and n == 1:
                            stats(2, 0)
                        if k == 3 and ahead:
                            stats(1, n + 2)
                if not first:
                    for k in range(5):
                        if isinstance(n, int) and n == 1:
                            parts = W2COUNT[k]
                            pe.wait_ge(wh2_done, parts)
                            pe.wait_ge(wl2_done, parts)
                        bank_free(2, n - 1, k, final=last)
                        conv_stream(2, n - 1, k)
                        if not last and k == (2 if prep else 1):
                            stats(2, n)

            pe.wait_ge(tab_loaded, 16)
            stats(1, 0)
            stats(1, 1)
            step(0, True, True, first=True)
            step(1, True, True)
            with pe.Fori(2, NP - 2) as n:
                step(n, True, True)
            step(NP - 2, True, False)
            step(NP - 1, False, False)
            step(NP, False, False, last=True)


def kernel(x, L0_conv_weight, L0_conv_bias, L1_conv_weight):
    import concourse.bacc as bacc
    from concourse.bass_utils import run_bass_kernel_spmd

    nc = bacc.Bacc("TRN2", target_bir_lowering=False, num_devices=1)
    arrays = {
        "x": np.ascontiguousarray(x),
        "w0": np.ascontiguousarray(L0_conv_weight),
        "bias": np.ascontiguousarray(L0_conv_bias),
        "w1": np.ascontiguousarray(L1_conv_weight),
        "tables": table_constants(),
    }
    args = [nc.dram_tensor(f"in_{k}", a.shape, mybir.dt.from_np(a.dtype), kind="ExternalInput").ap()
            for k, a in arrays.items()]
    out = nc.dram_tensor("out", (B, C, H, W), F32, kind="ExternalOutput").ap()
    build(nc, *args, out)
    r = run_bass_kernel_spmd(nc, [{f"in_{k}": a for k, a in arrays.items()}], core_ids=[0])
    return r.results[0]["out"]
```

```python
from contextlib import ExitStack

import numpy as np
import concourse.bass as bass
from concourse import mybir

ALU = mybir.AluOpType
ACT = mybir.ActivationFunctionType
AX_X, AX_XY = mybir.AxisListType.X, mybir.AxisListType.XY
F32 = mybir.dt.float32
F16 = mybir.dt.float16
BF16 = mybir.dt.bfloat16
I32 = mybir.dt.int32
RMAX = bass.bass_isa.ReduceOp.max

P = 128
B, C, H, W = 16, 32, 48, 48
RB = P // C
T = H // RB
IMG = 2
NP = B // IMG
PAIR = T * IMG * W
GROUPS = 16
N_GROUP = (C // GROUPS) * H * W
U = W // 3
OUTN = T * IMG * U
STREAMS = (1, 2, 0, 3, 4)
K1, K2 = 9, 5
PAD1 = 4
G1, G2 = 3, 2
GROUP_ORDER = (1, 0, 2)
KB1, KB2 = 3, 2
U1, U2 = U + G1 - 1, U + G2 - 1
W1 = 3 * (U1 - 1) + 5
W2 = W + 4
R1, R2 = T * IMG, (T + 1) * IMG
X_SCALE = 64.0
W_SCALE = 4096.0
OUT_FACTORS = (-1 / 2, 1 / 6, -1 / 6, 1 / 2, 1 / 6, 1 / 3, 2 / 3, 1.0)
EPS = 1e-5
ROUND = 12582912.0
ROOT_BITS = float(0x5F3759DF + 6 * 2**23)
TWO_PI = 6.2831850
NF = len(OUT_FACTORS)
NE = KB1 * RB
SPOS = {j: i + 1 for i, j in enumerate((3, 1, 2, 0, 4))}
PRESUM = (1, 2, 0, 4)
W2SRC = (5, 6, 0, 11, 0)
W2COUNT = (2, 4, 6, 8, 9)
SMALL = 10
WARMING = 13
ZDMA = 6


def table_constants():
    kr = np.arange(P)[:, None] // C
    e = np.arange(NE)[None, :]
    yy = (RB * (e // RB) - e % RB + kr - PAD1).astype(np.float32)
    mask = np.where(np.abs(yy) <= PAD1, 0.0, -1e30).astype(np.float32)
    grp = (np.arange(P) % C) // (C // GROUPS)
    gm = (grp[:, None] == grp[None, :]).astype(np.float32) / np.float32(N_GROUP)
    fac = np.tile(np.array(OUT_FACTORS) / (X_SCALE * W_SCALE), (P, 1))
    return np.concatenate([yy, yy * yy, mask, gm, fac], axis=1).astype(np.float32)


def build(nc, x, w0, bias, w1, tables, out):
    with ExitStack() as ctx:
        def sb(name, shape, dt=F32):
            return ctx.enter_context(nc.sbuf_tensor(name, shape, dt))

        def sem(name):
            return ctx.enter_context(nc.semaphore(name))

        X = sb("X", [P, NP * PAIR])
        P1 = sb("P1", [P, R1, W1])
        Z = sb("Z", [P, R2, W])
        P2 = sb("P2", [P, R2, W2])
        pre = {1: sb("pre1", [P, 4, R1 * U1]), 2: sb("pre2", [P, 4, R2 * U2])}
        s32 = {1: sb("s32_1", [P, 5, R1 * U1]), 2: sb("s32_2", [P, 5, R2 * U2])}
        hi = {1: sb("hi1", [P, 5, R1, U1], F16), 2: sb("hi2", [P, 5, R2, U2], F16)}
        lo = {1: sb("lo1", [P, 5, R1, U1], F16), 2: sb("lo2", [P, 5, R2, U2], F16)}
        wh = {1: sb("wh1", [P, 5, G1 * KB1 * P], F16), 2: sb("wh2", [P, 5, G2 * KB2 * P], F16)}
        wl = {1: sb("wl1", [P, 5, G1 * KB1 * P], F16), 2: sb("wl2", [P, 5, G2 * KB2 * P], F16)}
        m1b = {1: sb("m1b1", [P, OUTN]), 2: sb("m1b2", [P, OUTN])}
        psum_ = {1: sb("ps1", [P, OUTN]), 2: sb("ps2", [P, OUTN])}
        pdif = {1: sb("pd1", [P, OUTN]), 2: sb("pd2", [P, OUTN])}
        bias_c = {1: sb("bias1", [P, 1]), 2: sb("bias2", [P, 1])}
        warm = sb("warm", [P, 1])
        junk = sb("junk", [P, 2, T * W], BF16)
        sums = {1: sb("sums1", [P, 4]), 2: sb("sums2", [P, 4])}
        mom = {1: sb("mom1", [P, 2, IMG]), 2: sb("mom2", [P, 2, IMG])}
        msq = {1: sb("msq1", [P, IMG]), 2: sb("msq2", [P, IMG])}
        var = {1: sb("var1", [P, IMG]), 2: sb("var2", [P, IMG])}
        vare = {1: sb("vare1", [P, IMG]), 2: sb("vare2", [P, IMG])}
        std = {1: sb("std1", [P, IMG]), 2: sb("std2", [P, IMG])}
        rcp = {1: sb("rcp1", [P, IMG]), 2: sb("rcp2", [P, IMG])}
        gsc = {1: sb("gsc1", [P, IMG]), 2: sb("gsc2", [P, IMG])}
        gof = {1: sb("gof1", [P, IMG]), 2: sb("gof2", [P, IMG])}
        tab = sb("tab", [P, 3 * NE + P + NF])
        yy_t, yy2_t, mask_t = (tab[:, i * NE:(i + 1) * NE] for i in range(3))
        group_t = tab[:, 3 * NE:3 * NE + P]
        factor_t = tab[:, 3 * NE + P:]
        osc = {1: factor_t, 2: sb("osc2", [P, NF])}
        prm = sb("prm", [P, C, 3])
        turn = sb("turn", [P, 2, C])
        rnd = sb("rnd", [P, 2, C])
        rnd2 = sb("rnd2", [P, 2, C])
        frac = sb("frac", [P, 2, C])
        sc = sb("sc", [P, 2, C])
        scq = sb("scq", [P, 2, C])
        wq = sb("wq", [P, 2, C])
        q = sb("q", [P, 16, C])
        bt = sb("bt", [P, NE, C])
        ca = pre[2][:, :, 0:NE * C]

        def ca_rows(k):
            return ca[:, k - 1, :].rearrange("p (e o) -> p e o", o=C)

        ak = sb("ak", [P, 4, C])
        arg = sb("arg", [P, K1, NE * C])
        ker = arg
        gt = sb("gt", [P, 5, G1 * NE * C])
        ksg = sb("ksg", [P, G1, C])
        ksum = sb("ksum", [P, C])
        krec = sb("krec", [P, C])
        rs = sb("rs", [P, C])
        NW2 = KB2 * RB
        stage = sb("stage", [P, C, NW2 * K2])
        g2t = sb("g2t", [P, 8, NW2, C])
        wmax = sb("wmax", [P, 1])
        wall = sb("wall", [P, 1])
        wclamp = sb("wclamp", [P, 1])
        wpow = sb("wpow", [P, 1], I32)
        winv = sb("winv", [P, 1], I32)
        wsc = sb("wsc", [P, 1])

        banks = ctx.enter_context(nc.psum_tensor("banks", [P, 8, 512], F32))
        BANK = {1: (0, 1, 2, 3, 4), 2: (5, 6, 0, 1, 2)}
        BANK_LAST = (5, 6, 0, 3, 4)
        STAT = {1: banks[:, 7, 0:4], 2: banks[:, 7, 4:8]}

        x_loaded = [sem(f"x_loaded{i}") for i in range(IMG)]
        tab_loaded = sem("tab_loaded")
        prm_loaded = sem("prm_loaded")
        bias_loaded = sem("bias_loaded")
        stage_loaded = sem("stage_loaded")
        z_loaded = sem("z_loaded")
        stored = sem("stored")
        pads_zero = sem("pads_zero")
        stage_zero = sem("stage_zero")
        consts_set = sem("consts_set")
        sums_done = {1: sem("sums1_done"), 2: sem("sums2_done")}
        plain_sums = sem("plain_sums")
        stat_mm = {1: sem("stat1_mm"), 2: sem("stat2_mm")}
        small = {1: sem("small1"), 2: sem("small2")}
        root_steps = sem("root_steps")
        std_done = {1: sem("std1_done"), 2: sem("std2_done")}
        norm_done = {1: sem("norm1_done"), 2: sem("norm2_done")}
        pre_done = {1: sem("pre1_done"), 2: sem("pre2_done")}
        s_done = {1: sem("s1_done"), 2: sem("s2_done")}
        hi_done = {1: sem("hi1_done"), 2: sem("hi2_done")}
        lo_done = {1: sem("lo1_done"), 2: sem("lo2_done")}
        conv_mm = {1: sem("conv1_mm"), 2: sem("conv2_mm")}
        m1_read = {1: sem("m1_read1"), 2: sem("m1_read2")}
        mid_done = {1: sem("mid1_done"), 2: sem("mid2_done")}
        res_done = {1: sem("res1_done"), 2: sem("res2_done")}
        out_done = {1: sem("out1_done"), 2: sem("out2_done")}
        last_middle = sem("last_middle")
        dve_w = sem("dve_w")
        pool_w = sem("pool_w")
        exponents_pool = sem("exponents_pool")
        even_done = sem("even_done")
        sin_done = sem("sin_done")
        exp_done = sem("exp_done")
        wh1_done = sem("wh1_done")
        stream4_scaled = sem("stream4_scaled")
        wl1_done = sem("wl1_done")
        wh2_done = sem("wh2_done")
        wl2_done = sem("wl2_done")
        wmax_done = sem("wmax_done")

        def pair(n):
            return X[:, bass.ds(n * PAIR, PAIR)]

        def image(n, i):
            return pair(n).rearrange("p (t m x) -> p t m x", t=T, m=IMG)[:, :, i, :]

        def cols(n, v):
            return pair(n).rearrange("p (r u v) -> p (r u) v", u=U, v=3)[:, :, v]

        USED = {1: {0: (1, U1), 1: (1, U1 - 1), 2: (1, U1 - 1), 3: (0, U1), 4: (0, U1 - 1)},
                2: {0: (0, U2), 1: (0, U2), 2: (0, U2), 3: (0, U2), 4: (0, U2 - 1)}}
        NU = {1: U1, 2: U2}

        def dcol(c, k, j):
            lo_, hi_ = USED[c][j]
            return (P1 if c == 1 else P2)[:, :, 3 * lo_ + k:3 * (hi_ - 1) + k + 1:3]

        def tiles(buf, c, i, j):
            lo_, hi_ = USED[c][j]
            return buf[c][:, i, :].rearrange("p (r u) -> p r u", u=NU[c])[:, :, lo_:hi_]

        def half(buf, c, j):
            lo_, hi_ = USED[c][j]
            if j == 3 and c == 1:
                lo_, hi_ = 1, U1 - 1
            return buf[c][:, j, :, lo_:hi_]

        def full(c, j):
            if j == 3 and c == 1:
                return tiles(s32, 1, 3, 1)
            return tiles(s32, c, j, j)

        def tap2(k):
            return stage[:, :, :].rearrange("p o (e j) -> p e o j", j=K2)[:, :, :, K2 - 1 - k]

        def W2PARTS(j):
            return {0: ((0, tap2(0)), (1, tap2(3))),
                    1: ((0, g2t[:, 1, :, :]), (1, g2t[:, 2, :, :])),
                    2: ((0, g2t[:, 3, :, :]), (1, g2t[:, 4, :, :])),
                    3: ((0, g2t[:, 7, :, :]), (1, g2t[:, 6, :, :])),
                    4: ((0, tap2(2)),)}[j]

        def tap(k):
            return ker[:, :, :].rearrange("p (g k) e -> p g k e", k=3)[:, :, k, :]

        def per_row(v):
            return v.unsqueeze(2).to_broadcast([P, NE, C])

        def per_chan(v):
            return v.unsqueeze(1).to_broadcast([P, NE, C])

        centre = arg[:, PAD1, :].rearrange("p (e o) -> p e o", o=C)

        def gtv(i):
            return gt[:, i, :].rearrange("p (g e) -> p g e", g=G1)

        def per_output(v, rows):
            return v[:, :].unsqueeze(1).to_broadcast([P, rows, C])

        PADDED2 = ((1, 1 + W, 1, 0, W, 1), (0, W2, W2 - 1, 1, 3, 1), (W + 1, W + 3, 1, W - 2, W - 4, -1))

        block = ctx.enter_context(nc.Block())

        def wait(eng, s, v):
            if isinstance(v, int) and v <= 0:
                return
            eng.wait_ge(s, v)

        MARK = {}

        def pre_sum(nce, eng, c, n, i):
            j = PRESUM[i]
            a, b, op = ((1, 2, ALU.add), (1, 2, ALU.subtract), (0, 2, ALU.subtract), (4, 2, ALU.subtract))[i]
            if i == 0:
                eng.wait_ge(norm_done[c], IMG * (n + 1))
                wait(eng, s_done[c], 5 * n)
            nce.tensor_tensor(tiles(pre, c, i, j), dcol(c, a, j), dcol(c, b, j), op).then_inc(pre_done[c], 1)

        def addressed(eng):
            eng.nop(nofuse=True)
            eng.wait_ge(consts_set, 1)

        @block.sync
        def _(sp):
            def dram_image(dram, n, i):
                return dram[bass.ds(n * IMG + i, 1)].rearrange("m c (t k) x -> (m k) c t x", k=RB)

            def load(n):
                for i in range(IMG):
                    sp.dma_start(image(n, i), dram_image(x, n, i)).then_inc(x_loaded[i], 16)

            def loaded(n):
                for i in range(IMG):
                    sp.wait_ge(x_loaded[i], 16 * (n + 1))

            def store(n, last=False):
                for i in range(IMG):
                    if last:
                        sp.wait_ge(out_done[2], 5 * n + 2 + 3 * (i + 1))
                    elif i == 0:
                        sp.wait_ge(out_done[2], 5 * n + 5)
                    sp.dma_start(dram_image(out, n, i), image(n, i)).then_inc(stored, 16)

            def shift(n):
                RW = IMG * W
                zf = Z[:, :, :].rearrange("p r x -> p (r x)")
                src = pair(n)
                sp.wait_ge(out_done[1], 5 * n + 5)
                wait(sp, norm_done[2], n)
                sp.dma_start(zf[C:P, 0:PAIR], src[0:P - C, :]).then_inc(z_loaded, 16)
                sp.dma_start(zf[0:C, RW:RW + PAIR], src[P - C:P, :]).then_inc(z_loaded, 16)
                ends = ((0, 0, 1), (1, T, H - 2), (2, T, H - 3), (3, T, 2))
                for k, t, r in ends:
                    kr, tr = r % RB, r // RB
                    sp.dma_start(zf[k * C:(k + 1) * C, t * RW:(t + 1) * RW],
                                 src[kr * C:(kr + 1) * C, tr * RW:(tr + 1) * RW]).then_inc(z_loaded, 16)

            for k in range(2):
                sp.dma_start(prm[k * C:(k + 1) * C], w0.rearrange("o c j -> c o j")).then_inc(prm_loaded, 16)
            load(0)
            sp.wait_ge(stage_zero, 1)
            for k in range(RB):
                sp.dma_start(stage[k * C:(k + 1) * C, :, k * K2:k * K2 + K2 * K2],
                             w1.rearrange("o c i j -> c o (i j)")).then_inc(stage_loaded, 16)
            for k in range(RB):
                sp.dma_start(bias_c[1][k * C:(k + 1) * C, :], bias.rearrange("(o i) -> o i", i=1)).then_inc(bias_loaded, 16)
            loaded(0)
            load(1)
            loaded(1)
            load(2)

            def step(n, prefetch, last=False):
                if prefetch:
                    loaded(n + 2)
                    load(n + 3)
                if not last:
                    shift(n)
                if not (isinstance(n, int) and n == 0):
                    store(n - 1, last)

            step(0, True)
            step(1, True)
            with sp.Fori(2, NP - 3) as n:
                step(n, True)
            step(NP - 3, False)
            step(NP - 2, False)
            step(NP - 1, False)
            step(NP, False, last=True)
            sp.wait_ge(stored, 16 * IMG * NP)

        @block.vector
        def _(dve):
            count = [0]

            def done(ins):
                count[0] += 1
                ins.then_inc(dve_w, 1)

            def stage_end():
                dve.wait_ge(dve_w, count[0])

            tt, ts, stt = nc.vector.tensor_tensor, nc.vector.tensor_scalar, nc.vector.scalar_tensor_tensor

            def angles():
                dve.wait_ge(prm_loaded, 16 * RB)
                done(ts(turn[:, 0, :], prm[:, :, 2], 1.0 / 360.0, None, ALU.mult))
                done(ts(turn[:, 1, :], prm[:, :, 2], 1.0 / 360.0, 0.25, ALU.mult, ALU.add))
                stage_end()
                done(ts(rnd[:, :, :], turn[:, :, :], ROUND, None, ALU.add))
                stage_end()
                done(ts(rnd2[:, :, :], rnd[:, :, :], -ROUND, None, ALU.add))
                stage_end()
                done(tt(frac[:, :, :], turn[:, :, :], rnd2[:, :, :], ALU.subtract))
                MARK["angle"] = count[0]

            def covariance():
                mul = ALU.mult
                done(tt(wq[:, 0, :], prm[:, :, 0], prm[:, :, 0], mul))
                done(tt(wq[:, 1, :], prm[:, :, 1], prm[:, :, 1], mul))
                dve.wait_ge(sin_done, 1)
                done(tt(scq[:, :, :], sc[:, :, :], sc[:, :, :], mul))
                done(tt(q[:, 0, :], sc[:, 0, :], sc[:, 1, :], mul))
                stage_end()
                done(tt(q[:, 1, :], scq[:, 1, :], wq[:, 0, :], mul))
                done(tt(q[:, 2, :], scq[:, 0, :], wq[:, 1, :], mul))
                done(tt(q[:, 3, :], scq[:, 0, :], wq[:, 0, :], mul))
                done(tt(q[:, 4, :], scq[:, 1, :], wq[:, 1, :], mul))
                done(tt(q[:, 5, :], wq[:, 0, :], wq[:, 1, :], ALU.subtract))
                stage_end()
                done(tt(q[:, 6, :], q[:, 1, :], q[:, 2, :], ALU.add))
                done(tt(q[:, 7, :], q[:, 3, :], q[:, 4, :], ALU.add))
                done(tt(q[:, 8, :], q[:, 0, :], q[:, 5, :], mul))
                stage_end()
                done(tt(q[:, 9, :], q[:, 6, :], q[:, 7, :], mul))
                done(tt(q[:, 10, :], q[:, 8, :], q[:, 8, :], mul))
                stage_end()
                done(tt(q[:, 11, :], q[:, 9, :], q[:, 10, :], ALU.subtract))
                stage_end()
                done(nc.vector.reciprocal(q[:, 12, :], q[:, 11, :]))
                stage_end()
                done(stt(q[:, 13, :], q[:, 7, :], -0.5, q[:, 12, :], mul, mul))
                done(tt(q[:, 14, :], q[:, 8, :], q[:, 12, :], mul))
                done(stt(q[:, 15, :], q[:, 6, :], -0.5, q[:, 12, :], mul, mul))
                stage_end()
                MARK["quadratic"] = count[0]

            def exponents():
                mul = ALU.mult
                dve.wait_ge(tab_loaded, 16)

                done(tt(centre, per_row(yy2_t), per_chan(q[:, 15, :]), mul))
                for k in range(1, 5):
                    done(ts(ak[:, k - 1, :], q[:, 13, :], float(k * k), None, mul))
                stage_end()
                done(tt(centre, centre, per_row(mask_t), ALU.add))
                stage_end()
                MARK["centre"] = count[0]
                btf = bt[:, :, :].rearrange("p e o -> p (e o)")
                taps = iter(range(1 - PAD1, K1))

                def next_exponent():
                    t = next(taps, None)
                    if t is None:
                        return
                    if t < 0:
                        done(tt(ca_rows(-t), centre, per_chan(ak[:, -t - 1, :]), ALU.add))
                        MARK["offset", -t] = count[0]
                        return
                    if t == PAD1:
                        t = next(taps)
                    k = t - PAD1
                    if abs(k) == PAD1:
                        dve.wait_ge(exponents_pool, 2)
                    else:
                        dve.wait_ge(dve_w, MARK["offset", abs(k)])
                    done(stt(arg[:, t, :], btf, float(k), ca[:, abs(k) - 1, :], mul, ALU.add))
                    if t % 3 == 2:
                        MARK["exponents", t // 3] = count[0]

                first_stats(next_exponent)
                for _ in range(K1):
                    next_exponent()

            def kernel_group(g):
                dve.wait_ge(even_done, g + 1)
                done(tt(gtv(1)[:, g], gtv(0)[:, g], tap(1)[:, g], ALU.add))
                stage_end()
                done(nc.vector.tensor_reduce(ksg[:, g, :], gtv(1)[:, g].rearrange("p (r o) -> p o r", o=C), AX_X, ALU.add))
                stage_end()
                if g > 0:
                    done(tt(ksum[:, :], ksg[:, 0, :] if g == 1 else ksum[:, :], ksg[:, g, :], ALU.add))

            def kernel_scale():
                stage_end()
                done(nc.vector.reciprocal(krec[:, :], ksum[:, :]))
                stage_end()

            def scaled(j, g, src):
                dst = gtv(j)[:, g].rearrange("p (r o) -> p r o", o=C)
                done(stt(dst, src[:, g].rearrange("p (r o) -> p r o", o=C), W_SCALE, per_output(krec, NE), ALU.mult, ALU.mult))
                MARK["scaled", j, g] = count[0]

            def scale_stream1():
                for g in GROUP_ORDER:
                    scaled(1, g, gtv(1))
                done(ts(rs[:, :], krec[:, :], W_SCALE, None, ALU.mult))

            def kernel_stream2():
                for g in GROUP_ORDER:
                    done(tt(gtv(2)[:, g], tap(1)[:, g], gtv(0)[:, g], ALU.subtract))
                for i, g in enumerate(GROUP_ORDER):
                    if i == 0:
                        stage_end()
                    scaled(2, g, gtv(2))

            def kernel_stream0():
                for g in GROUP_ORDER:
                    scaled(0, g, tap(0))

            def kernel_stream3():
                done(stt(gtv(4), tap(1), 2.0, tap(0), ALU.mult, ALU.add))
                stage_end()
                done(stt(gtv(3), tap(2), 4.0, gtv(4), ALU.mult, ALU.add))
                stage_end()
                MARK["free", 4] = count[0]
                for g in GROUP_ORDER:
                    scaled(3, g, gtv(3))

            def layer2_largest():
                dve.wait_ge(stage_loaded, 16 * RB)
                done(nc.vector.tensor_reduce(wmax[:, :], stage[:, :, :].rearrange("p o e -> p (o e)"), AX_X, ALU.max,
                                             apply_absolute_value=True))
                MARK["largest2"] = count[0]

            def layer2_scale():
                dve.wait_ge(wmax_done, 1)
                done(ts(wclamp[:, :], wall[:, :], 1e-30, None, ALU.max))
                stage_end()
                done(ts(wpow[:, :], wclamp[:, :].bitcast(I32), 0x7F800000, None, ALU.bitwise_and))
                stage_end()
                done(ts(winv[:, :], wpow[:, :], -1.0, float(0x7F000000), ALU.mult, ALU.add))
                done(ts(osc[2][:, :], factor_t, wpow[:, :].bitcast(F32), None, ALU.mult))
                stage_end()
                done(ts(wsc[:, :], winv[:, :].bitcast(F32), W_SCALE, None, ALU.mult))
                stage_end()
                MARK["scale2"] = count[0]

            def low_layer2():
                m = 0
                for k in range(5):
                    j = STREAMS[k]
                    dve.wait_ge(pool_w, W2SRC[k])
                    for g, src in W2PARTS(j):
                        m += 1
                        dve.wait_ge(wh2_done, m)
                        sl = slice(g * NW2 * C, (g + 1) * NW2 * C)
                        stt(wl[2][:, j, sl].rearrange("p (e o) -> p e o", o=C), src, wsc[:, 0:1],
                            wh[2][:, j, sl].rearrange("p (e o) -> p e o", o=C), ALU.mult, ALU.subtract).then_inc(wl2_done, 1)

            def first_stats(fill):
                mean, ex2 = mom[1][:, 0, :], mom[1][:, 1, :]
                steps = [0]

                def landed(ins):
                    steps[0] += 1
                    ins.then_inc(root_steps, 1)
                    fill()
                    dve.wait_ge(root_steps, steps[0])

                dve.wait_ge(stat_mm[1], 1)
                landed(nc.vector.tensor_copy(mom[1][:, :, :].rearrange("p a b -> p (a b)"), STAT[1]))
                landed(stt(msq[1][:, :], mean, -1.0, mean, ALU.mult, ALU.mult))
                landed(tt(var[1][:, :], ex2, msq[1][:, :], ALU.add))
                landed(ts(vare[1][:, :], var[1][:, :], 0.0, EPS, ALU.max, ALU.add))
                landed(ts(rcp[1][:, :].bitcast(I32), vare[1][:, :].bitcast(I32), -0.5, ROOT_BITS, ALU.mult, ALU.add))
                for _ in range(3):
                    landed(stt(msq[1][:, :], vare[1][:, :], -0.5 / (X_SCALE * X_SCALE), rcp[1][:, :], ALU.mult, ALU.mult))
                    landed(tt(var[1][:, :], msq[1][:, :], rcp[1][:, :], ALU.mult))
                    landed(stt(rcp[1][:, :], var[1][:, :], 1.5, rcp[1][:, :], ALU.add, ALU.mult))
                nc.vector.tensor_copy(gsc[1][:, :], rcp[1][:, :]).then_inc(small[1], SMALL - 1)
                stt(gof[1][:, :], mean, -1.0, rcp[1][:, :], ALU.mult, ALU.mult).then_inc(small[1], 1)

            def small_stats(c, n):
                dve.wait_ge(stat_mm[c], n + 1)
                wait(dve, norm_done[c], IMG * n)
                nc.vector.tensor_copy(mom[c][:, :, :].rearrange("p a b -> p (a b)"), STAT[c]).then_inc(small[c], 1)
                mean, ex2 = mom[c][:, 0, :], mom[c][:, 1, :]
                at = SMALL * n
                dve.wait_ge(small[c], at + 1)
                stt(msq[c][:, :], mean, -1.0, mean, ALU.mult, ALU.mult).then_inc(small[c], 1)
                dve.wait_ge(small[c], at + 2)
                tt(var[c][:, :], ex2, msq[c][:, :], ALU.add).then_inc(small[c], 1)
                dve.wait_ge(small[c], at + 3)
                ts(vare[c][:, :], var[c][:, :], 0.0, EPS, ALU.max, ALU.add).then_inc(small[c], 1)
                dve.wait_ge(std_done[c], n + 1 if c == 2 else n)
                nc.vector.reciprocal(rcp[c][:, :], std[c][:, :]).then_inc(small[c], 1)
                dve.wait_ge(small[c], at + 5)
                stt(msq[c][:, :], vare[c][:, :], 1.0 / (X_SCALE * X_SCALE), rcp[c][:, :], ALU.mult, ALU.mult).then_inc(small[c], 1)
                dve.wait_ge(small[c], at + 6)
                tt(var[c][:, :], msq[c][:, :], rcp[c][:, :], ALU.mult).then_inc(small[c], 1)
                dve.wait_ge(small[c], at + 7)
                ts(msq[c][:, :], var[c][:, :], -0.5, 1.5, ALU.mult, ALU.add).then_inc(small[c], 1)
                dve.wait_ge(small[c], at + 8)
                tt(gsc[c][:, :], msq[c][:, :], rcp[c][:, :], ALU.mult).then_inc(small[c], 1)
                dve.wait_ge(small[c], at + 9)
                stt(gof[c][:, :], mean, -1.0, gsc[c][:, :], ALU.mult, ALU.mult).then_inc(small[c], 1)

            def last_plain_sums():
                dve.wait_ge(out_done[1], 5 * NP)
                dve.wait_ge(stat_mm[2], NP - 1)
                for i in range(IMG):
                    nc.vector.tensor_reduce(sums[2][:, i:i + 1], image(NP - 1, i), AX_XY, ALU.add).then_inc(plain_sums, 1)

            def last_normalise():
                n, i = NP - 1, IMG - 1
                dve.wait_ge(small[2], SMALL * NP)
                dve.wait_ge(z_loaded, ZDMA * 16 * NP)
                dve.wait_ge(pre_done[2], 4 * n)
                src = Z[:, :, :].rearrange("p (t m) x -> p t m x", m=IMG)[:, :, i, :]
                dst = P2[:, :, :].rearrange("p (t m) x -> p t m x", m=IMG)[:, :, i, :]
                for d0, d1, ds_, s0, s1, ss in PADDED2:
                    ins = ts(dst[:, :, d0:d1:ds_], src[:, :, s0:s1:ss], gsc[2][:, i:i + 1], gof[2][:, i:i + 1],
                             ALU.mult, ALU.add)
                ins.then_inc(norm_done[2], 1)

            def stream3(c, n):
                dve.wait_ge(norm_done[c], IMG * (n + 1))
                wait(dve, lo_done[c], 5 * n)
                tt(tiles(s32, c, 3, 3), dcol(c, 3, 3), dcol(c, 1, 3), ALU.subtract).then_inc(s_done[c], 1)

            def make_stream(c, n, i):
                j = PRESUM[i]
                dve.wait_ge(pre_done[c], 4 * n + i + 1)
                if i == 0:
                    dve.wait_ge(s_done[c], 5 * n + 1)
                a, t_, dst = tiles(s32, c, 3, j), tiles(pre, c, i, j), tiles(s32, c, j, j)
                if j == 1:
                    tt(dst, a, t_, ALU.subtract).then_inc(s_done[c], 1)
                elif j == 2:
                    stt(dst, t_, 3.0, a, ALU.mult, ALU.add).then_inc(s_done[c], 1)
                elif j == 0:
                    stt(dst, t_, 2.0, a, ALU.mult, ALU.add).then_inc(s_done[c], 1)
                else:
                    stt(dst, a, -2.0, t_, ALU.mult, ALU.add).then_inc(s_done[c], 1)

            def low_half(c, n, k):
                j = STREAMS[k]
                dve.wait_ge(hi_done[c], 5 * n + k + 1)
                tt(half(lo, c, j), full(c, j), half(hi, c, j), ALU.subtract).then_inc(lo_done[c], 1)

            def own_stream(c, n, i):
                pre_sum(nc.vector, dve, c, n, i)
                make_stream(c, n, i)

            def product(c, k):
                return banks[:, BANK[c][k], 0:OUTN]

            def middle(c, n):
                dve.wait_ge(conv_mm[c], 5 * n + 2)
                dve.wait_ge(m1_read[c], n + 1)
                wait(dve, res_done[c], 3 * n)
                stt(psum_[c][:, :], product(c, 1), osc[c][:, 1:2], m1b[c][:, :], ALU.mult, ALU.add).then_inc(mid_done[c], 1)
                stt(pdif[c][:, :], product(c, 1), osc[c][:, 2:3], m1b[c][:, :], ALU.mult, ALU.add).then_inc(mid_done[c], 1)

            def add_m0(c, n):
                dve.wait_ge(conv_mm[c], 5 * n + 3)
                dve.wait_ge(res_done[c], 3 * n + 1)
                stt(cols(n, 0), product(c, 2), osc[c][:, 3:4], cols(n, 0), ALU.mult, ALU.add).then_inc(out_done[c], 1)

            def add_m3_to(c, n, v):
                if v == 1:
                    dve.wait_ge(conv_mm[c], 5 * n + 4)
                    dve.wait_ge(res_done[c], 3 * n + 3)
                if v == 0:
                    dve.wait_ge(out_done[c], 5 * n + 1)
                f = 4 + v
                stt(cols(n, v), product(c, 3), osc[c][:, f:f + 1], cols(n, v), ALU.mult, ALU.add).then_inc(out_done[c], 1)

            def add_m3(c, n):
                for v in (1, 2, 0):
                    add_m3_to(c, n, v)

            def last_output():
                n, f = NP - 1, osc[2]
                m3, m4 = (banks[:, BANK_LAST[k], 0:OUTN].rearrange("p (t m u) -> p t m u", m=IMG, u=U) for k in (3, 4))
                dve.wait_ge(conv_mm[2], 5 * n + 4)
                dve.wait_ge(last_middle, 1)
                stt(cols(n, 2), banks[:, BANK_LAST[3], 0:OUTN], f[:, 6:7], cols(n, 2), ALU.mult, ALU.add).then_inc(out_done[2], 1)
                dve.wait_ge(res_done[2], 3 * n + 2)
                dve.wait_ge(out_done[2], 5 * n + 1)
                for i in range(IMG):
                    y = [image(n, i)[:, :, v::3] for v in range(3)]
                    for v in (0, 1):
                        stt(y[v], m3[:, :, i, :], f[:, 4 + v:5 + v], y[v], ALU.mult, ALU.add).then_inc(out_done[2], 1)
                    if i == 0:
                        dve.wait_ge(conv_mm[2], 5 * NP)
                        dve.wait_ge(out_done[2], 5 * n + 2)
                    stt(y[2], m4[:, :, i, :], f[:, 7:8], y[2], ALU.mult, ALU.add).then_inc(out_done[2], 1)

            def last_residual():
                dve.wait_ge(mid_done[2], 2 * NP - 1)
                tt(cols(NP - 1, 2), cols(NP - 1, 2), psum_[2][:, :], ALU.add).then_inc(last_middle, 1)

            def add_m4(c, n):
                dve.wait_ge(conv_mm[c], 5 * n + 5)
                dve.wait_ge(out_done[c], 5 * n + 3)
                stt(cols(n, 2), product(c, 4), osc[c][:, 7:8], cols(n, 2), ALU.mult, ALU.add).then_inc(out_done[c], 1)

            angles()
            covariance()
            exponents()
            for g in range(G1):
                kernel_group(g)
            stream3(1, 0)
            make_stream(1, 0, 0)
            kernel_scale()
            scale_stream1()
            low_half(1, 0, 0)
            make_stream(1, 0, 1)
            kernel_stream2()
            low_half(1, 0, 1)
            kernel_stream0()
            make_stream(1, 0, 2)
            low_half(1, 0, 2)
            kernel_stream3()
            make_stream(1, 0, 3)
            low_half(1, 0, 3)
            low_half(1, 0, 4)
            middle(1, 0)
            small_stats(1, 1)
            layer2_largest()

            def streams_ahead(c, n):
                stream3(c, n)
                make_stream(c, n, 0)
                make_stream(c, n, 1)
                low_half(c, n, 0)
                make_stream(c, n, 2)
                low_half(c, n, 1)
                make_stream(c, n, 3)

            def layer1_streams(n):
                stream3(1, n)
                for i in range(4):
                    make_stream(1, n, i)

            def low_halves(c, n, ks):
                for k in ks:
                    low_half(c, n, k)

            def first_step():
                stream3(1, 1)
                for i in range(4):
                    own_stream(1, 1, i)
                low_half(1, 1, 0)
                layer2_scale()
                add_m0(1, 0)
                add_m3(1, 0)
                add_m4(1, 0)
                low_half(1, 1, 1)
                small_stats(1, 2)
                low_halves(1, 1, range(2, 5))
                small_stats(2, 0)
                middle(1, 1)
                low_layer2()

            def second_step():
                add_m0(1, 1)
                streams_ahead(2, 0)
                add_m3(1, 1)
                low_half(2, 0, 2)
                small_stats(1, 3)
                add_m4(1, 1)
                low_halves(2, 0, range(3, 5))
                middle(2, 0)
                stream3(1, 2)
                make_stream(1, 2, 0)
                make_stream(1, 2, 1)
                add_m0(2, 0)
                low_half(1, 2, 0)
                make_stream(1, 2, 2)
                make_stream(1, 2, 3)
                low_half(1, 2, 1)
                small_stats(2, 1)
                add_m3(2, 0)
                low_halves(1, 2, range(2, 5))
                add_m4(2, 0)

            def step(n, ahead=True):
                streams_ahead(2, n - 1)
                low_halves(2, n - 1, range(2, 5))
                middle(1, n)
                add_m0(1, n)
                if ahead:
                    small_stats(1, n + 2)
                add_m3(1, n)
                add_m4(1, n)
                layer1_streams(n + 1)
                middle(2, n - 1)
                low_halves(1, n + 1, range(5))
                add_m0(2, n - 1)
                small_stats(2, n)
                add_m3(2, n - 1)
                add_m4(2, n - 1)

            def last_steps():
                n = NP - 1
                streams_ahead(2, n - 1)
                low_halves(2, n - 1, range(2, 5))
                middle(1, n)
                add_m0(1, n)
                add_m3(1, n)
                add_m4(1, n)
                last_plain_sums()
                small_stats(2, n)
                middle(2, n - 1)
                last_normalise()
                add_m0(2, n - 1)
                stream3(2, n)
                own_stream(2, n, 0)
                for i, v in ((1, 1), (2, 2), (3, 0)):
                    add_m3_to(2, n - 1, v)
                    low_half(2, n, i - 1)
                    make_stream(2, n, i)
                add_m4(2, n - 1)
                low_half(2, n, 3)
                middle(2, n)
                low_half(2, n, 4)
                last_residual()
                add_m0(2, n)
                last_output()

            first_step()
            second_step()
            with dve.Fori(2, NP - 2) as n:
                step(n)
            step(NP - 2, ahead=False)
            last_steps()

        @block.scalar
        def _(act):
            for k in range(2, RB):
                act.dma_start(prm[k * C:(k + 1) * C], w0.rearrange("o c j -> c o j")).then_inc(prm_loaded, 16)
            act.dma_start(tab[:, :], tables).then_inc(tab_loaded, 16)

            def channel_sums(c, n, shared=False):
                if c == 2:
                    act.wait_ge(out_done[1], 5 * n + 5)
                wait(act, stat_mm[c], n)
                waste = junk[:, c - 1, :].rearrange("p (t x) -> p t x", t=T)
                kinds = ((1, ACT.Square),) if shared else ((0, ACT.Identity), (1, ACT.Square))
                count = 0
                for i in range(IMG):
                    if c == 1:
                        act.wait_ge(x_loaded[i], 16 * (n + 1))
                    for kind, function in kinds:
                        wait(act, sums_done[c], 2 * IMG * n + count)
                        addressed(act)
                        col = IMG * kind + i
                        nc.scalar.activation(waste, image(n, i), function,
                                             accum_out=sums[c][:, col:col + 1]).then_inc(sums_done[c], 1)
                        count += 1

            def standard_deviation(c, n):
                act.wait_ge(small[c], SMALL * n + 4)
                nc.scalar.activation(std[c][:, :], vare[c][:, :], ACT.Sqrt,
                                     scale=1.0 / (X_SCALE * X_SCALE)).then_inc(std_done[c], 1)

            def normalise1(n):
                act.wait_ge(small[1], SMALL * (n + 1))
                wait(act, s_done[1], 5 * n)
                wait(act, pre_done[1], 4 * n)
                act.wait_ge(pads_zero, 1)
                addressed(act)
                for i in range(IMG):
                    dst = P1[:, :, :].rearrange("p (t m) x -> p t m x", m=IMG)[:, :, i, PAD1:PAD1 + W]
                    nc.scalar.activation(dst, image(n, i), ACT.Identity, bias=gof[1][:, i:i + 1],
                                         scale=gsc[1][:, i:i + 1]).then_inc(norm_done[1], 1)

            def normalise2(n, shared=False):
                act.wait_ge(small[2], SMALL * (n + 1))
                act.wait_ge(z_loaded, ZDMA * 16 * (n + 1))
                wait(act, s_done[2], 5 * n)
                wait(act, pre_done[2], 4 * n)
                for i in range(IMG - 1 if shared else IMG):
                    src = Z[:, :, :].rearrange("p (t m) x -> p t m x", m=IMG)[:, :, i, :]
                    dst = P2[:, :, :].rearrange("p (t m) x -> p t m x", m=IMG)[:, :, i, :]
                    for d0, d1, ds_, s0, s1, ss in PADDED2:
                        ins = nc.scalar.activation(dst[:, :, d0:d1:ds_], src[:, :, s0:s1:ss], ACT.Identity,
                                                   bias=gof[2][:, i:i + 1], scale=gsc[2][:, i:i + 1])
                    ins.then_inc(norm_done[2], 1)

            def high_half(c, n, k):
                j = STREAMS[k]
                act.wait_ge(s_done[c], 5 * n + SPOS[j])
                wait(act, conv_mm[c], 5 * n + k + 1 - 5)
                nc.scalar.copy(half(hi, c, j), full(c, j)).then_inc(hi_done[c], 1)

            def read_m1(c, n):
                act.wait_ge(conv_mm[c], 5 * n + 1)
                wait(act, mid_done[c], 2 * n)
                nc.scalar.activation(m1b[c][:, :], banks[:, BANK[c][0], 0:OUTN], ACT.Identity,
                                     bias=bias_c[c][:, 0:1], scale=osc[c][:, 0:1]).then_inc(m1_read[c], 1)

            def high_kernel(k):
                j = STREAMS[k]
                if j == 4:
                    act.wait_ge(stream4_scaled, 1)
                for g in GROUP_ORDER:
                    if j != 4:
                        act.wait_ge(dve_w, MARK["scaled", j, g])
                    at = slice(g * NE * C, (g + 1) * NE * C)
                    nc.scalar.copy(wh[1][:, j, at], gt[:, j, at]).then_inc(wh1_done, 1)

            def high_layer2():
                for k in range(5):
                    j = STREAMS[k]
                    act.wait_ge(pool_w, W2SRC[k])
                    act.wait_ge(dve_w, MARK["scale2"])
                    for g, src in W2PARTS(j):
                        ins = nc.scalar.mul(wh[2][:, j, g * NW2 * C:(g + 1) * NW2 * C].rearrange("p (e o) -> p e o", o=C),
                                            src, wsc[:, 0:1])
                        ins.then_inc(wh2_done, 1)

            act.wait_ge(dve_w, MARK["angle"])
            nc.scalar.activation(sc[:, :, :], frac[:, :, :], ACT.Sin, scale=TWO_PI).then_inc(sin_done, 1)
            channel_sums(1, 0)
            act.wait_ge(consts_set, 1)
            nc.scalar.activation(warm[:, :], bias_c[2][:, :], ACT.Exp)
            for g in range(G1):
                act.wait_ge(dve_w, MARK["exponents", g])
                nc.scalar.activation(ker[:, 3 * g:3 * g + 3, :], arg[:, 3 * g:3 * g + 3, :], ACT.Exp).then_inc(exp_done, 1)
                if g == 2:
                    normalise1(0)
            high_half(1, 0, 0)
            high_kernel(0)
            high_half(1, 0, 1)
            high_kernel(1)
            high_kernel(2)
            high_half(1, 0, 2)
            high_half(1, 0, 3)
            channel_sums(1, 1)
            high_kernel(3)
            high_half(1, 0, 4)
            act.wait_ge(bias_loaded, 16 * RB)
            read_m1(1, 0)
            standard_deviation(1, 1)
            high_kernel(4)

            def high_halves(c, n, ks):
                for k in ks:
                    high_half(c, n, k)

            def first_step():
                normalise1(1)
                channel_sums(1, 2)
                high_halves(1, 1, range(5))
                high_layer2()
                standard_deviation(1, 2)
                channel_sums(2, 0)
                standard_deviation(2, 0)
                read_m1(1, 1)

            def second_step():
                normalise2(0)
                normalise1(2)
                channel_sums(1, 3)
                high_halves(2, 0, range(5))
                standard_deviation(1, 3)
                read_m1(2, 0)
                channel_sums(2, 1)
                high_halves(1, 2, range(5))
                standard_deviation(2, 1)

            def step(n, ahead=True):
                normalise2(n - 1)
                normalise1(n + 1)
                high_halves(2, n - 1, range(2))
                read_m1(1, n)
                high_halves(2, n - 1, range(2, 5))
                if ahead:
                    channel_sums(1, n + 2)
                    standard_deviation(1, n + 2)
                channel_sums(2, n)
                read_m1(2, n - 1)
                high_halves(1, n + 1, range(5))
                standard_deviation(2, n)

            def last_steps():
                n = NP - 1
                normalise2(n - 1)
                high_halves(2, n - 1, range(2))
                read_m1(1, n)
                high_halves(2, n - 1, range(2, 5))
                channel_sums(2, n, shared=True)
                standard_deviation(2, n)
                read_m1(2, n - 1)
                normalise2(n, shared=True)
                high_halves(2, n, range(5))
                read_m1(2, n)

            first_step()
            second_step()
            with act.Fori(2, NP - 2) as n:
                step(n)
            step(NP - 2, ahead=False)
            last_steps()

        @block.gpsimd
        def _(pool):
            nc.gpsimd.memset(stage[:, :, :], 0.0).then_inc(stage_zero, 1)
            nc.gpsimd.memset(P1[:, :, :], 0.0).then_inc(pads_zero, 1)
            nc.gpsimd.memset(bias_c[2][:, :], 0.0).then_inc(consts_set, 1)

            tt, ts = nc.gpsimd.tensor_tensor, nc.gpsimd.tensor_scalar
            count = [0]

            def done(ins):
                count[0] += 1
                ins.then_inc(pool_w, 1)

            def stage_end():
                pool.wait_ge(pool_w, count[0])

            def exponent_terms():
                pool.wait_ge(tab_loaded, 16)
                pool.wait_ge(dve_w, MARK["quadratic"])
                tt(bt[:, :, :], per_row(yy_t), per_chan(q[:, 14, :]), ALU.mult).then_inc(exponents_pool, 1)
                pool.wait_ge(dve_w, MARK["centre"])
                tt(ca_rows(4), centre, per_chan(ak[:, 3, :]), ALU.add).then_inc(exponents_pool, 1)

            def even_taps(g):
                pool.wait_ge(exp_done, g + 1)
                tt(gtv(0)[:, g], tap(0)[:, g], tap(2)[:, g], ALU.add).then_inc(even_done, 1)

            def layer2_taps1():
                pool.wait_ge(stage_loaded, 16 * RB)
                done(tt(g2t[:, 0, :, :], tap2(0), tap2(2), ALU.add))
                done(tt(g2t[:, 2, :, :], tap2(3), tap2(4), ALU.add))
                done(tt(g2t[:, 4, :, :], tap2(4), tap2(3), ALU.subtract))

            def layer2_taps2():
                done(ts(g2t[:, 7, :, :], tap2(1), 2.0, None, ALU.mult))

            def layer2_taps3():
                stage_end()
                done(tt(g2t[:, 1, :, :], g2t[:, 0, :, :], tap2(1), ALU.add))
                done(tt(g2t[:, 3, :, :], tap2(1), g2t[:, 0, :, :], ALU.subtract))

            def layer2_taps4():
                done(tt(g2t[:, 5, :, :], g2t[:, 7, :, :], tap2(0), ALU.add))
                done(ts(g2t[:, 0, :, :], tap2(2), 4.0, None, ALU.mult))
                stage_end()
                done(tt(g2t[:, 7, :, :], g2t[:, 5, :, :], g2t[:, 0, :, :], ALU.add))
                stage_end()
                done(ts(g2t[:, 5, :, :], tap2(4), 2.0, None, ALU.mult))
                stage_end()
                done(tt(g2t[:, 6, :, :], g2t[:, 5, :, :], tap2(3), ALU.add))
                assert count[0] == W2SRC[3], count[0]

            def pre_sums(c, n):
                for i in range(4):
                    pre_sum(nc.gpsimd, pool, c, n, i)

            def scale_stream4():
                pool.wait_ge(dve_w, MARK["free", 4])
                for g in range(G1):
                    src = tap(2)[:, g, :].rearrange("p (e o) -> p e o", o=C)
                    ins = tt(gtv(4)[:, g, :].rearrange("p (e o) -> p e o", o=C), src, per_output(rs, NE), ALU.mult)
                ins.then_inc(stream4_scaled, 1)

            def low_kernel(k):
                j = STREAMS[k]
                if j == 4:
                    pool.wait_ge(stream4_scaled, 1)
                if k < 2:
                    for i, g in enumerate(GROUP_ORDER):
                        pool.wait_ge(wh1_done, G1 * k + i + 1)
                        at = slice(g * NE * C, (g + 1) * NE * C)
                        tt(wl[1][:, j, at], gt[:, j, at], wh[1][:, j, at], ALU.subtract).then_inc(wl1_done, 1)
                else:
                    pool.wait_ge(wh1_done, G1 * (k + 1))
                    tt(wl[1][:, j, :], gt[:, j, :], wh[1][:, j, :], ALU.subtract).then_inc(wl1_done, G1)

            def residual(c, n):
                last = c == 2 and isinstance(n, int) and n == NP - 1
                columns = ((0, psum_), (1, pdif)) if last else ((0, psum_), (1, pdif), (2, psum_))
                for i, (v, src) in enumerate(columns):
                    if i == 0:
                        pool.wait_ge(mid_done[c], 2 * n + 1)
                        if c == 1:
                            pool.wait_ge(norm_done[1], IMG * (n + 1))
                        else:
                            pool.wait_ge(z_loaded, ZDMA * 16 * (n + 1))
                            pool.wait_ge(sums_done[2], 2 * IMG * (n + 1) - (IMG if last else 0))
                            if last:
                                pool.wait_ge(plain_sums, IMG)
                    if i == 1:
                        pool.wait_ge(mid_done[c], 2 * n + 2)
                    addressed(pool)
                    tt(cols(n, v), cols(n, v), src[c][:, :], ALU.add).then_inc(res_done[c], 1)

            exponent_terms()
            layer2_taps1()
            even_taps(0)
            even_taps(1)
            even_taps(2)
            pool.wait_ge(pads_zero, 1)
            pre_sums(1, 0)
            low_kernel(0)
            layer2_taps2()
            low_kernel(1)
            low_kernel(2)
            layer2_taps3()
            scale_stream4()
            low_kernel(3)
            low_kernel(4)
            pool.wait_ge(dve_w, MARK["largest2"])
            nc.gpsimd.partition_all_reduce(wall[:, :], wmax[:, :], P, RMAX).then_inc(wmax_done, 1)

            def step(n, prep, first=False, last=False):
                early = isinstance(n, int) and n < 2
                if early:
                    residual(1, n)
                if first:
                    layer2_taps4()
                if not first and not last:
                    pre_sums(2, n - 1)
                if not last and not early:
                    residual(1, n)
                if prep and not first:
                    pre_sums(1, n + 1)
                if last:
                    pool.wait_ge(pre_done[2], 4 * (n - 1) + 1)
                    for i in range(1, 4):
                        pre_sum(nc.gpsimd, pool, 2, n - 1, i)
                if not first:
                    residual(2, n - 1)

            step(0, True, first=True)
            step(1, True)
            with pool.Fori(2, NP - 1) as n:
                step(n, True)
            step(NP - 1, False)
            step(NP, False, last=True)

        @block.tensor
        def _(pe):
            KB = {1: KB1, 2: KB2}
            G = {1: G1, 2: G2}

            def stats(c, n, shared=False):
                pe.wait_ge(sums_done[c], 2 * IMG * (n + 1) - (IMG if shared else 0))
                if shared:
                    pe.wait_ge(plain_sums, IMG)
                nc.tensor.matmul(STAT[c], group_t, sums[c][:, :], start=True, stop=True).then_inc(stat_mm[c], 1)

            def spans(c, j, g, b):
                if c == 2:
                    return (0, R1), (IMG * b, IMG * b + R1), (0, U)
                rows_out = ((IMG, R1), (0, R1), (0, R1 - IMG))[b]
                rows_in = ((0, R1 - IMG), (0, R1), (IMG, R1))[b]
                u0 = 1 if g == 0 and j != 4 else 0
                u1 = U - 1 if g == G1 - 1 and j != 0 else U
                return rows_out, rows_in, (u0, u1)

            def conv_stream(c, n, k, first=False, final=False):
                j = STREAMS[k]
                groups = 1 if (c == 2 and j == 4) else G[c]
                steps = [(g, b) for g in range(groups) for b in range(KB[c])]
                if c == 1:
                    steps.sort(key=lambda gb: (GROUP_ORDER.index(gb[0]), gb != (1, 1)))
                dst = banks[:, (BANK_LAST if final else BANK[c])[k], 0:OUTN].rearrange("p (r u) -> p r u", u=U)
                parts = ((wh, hi), (wh, lo), (wl, hi))
                for part, (wbuf, xbuf) in enumerate(parts):
                    if part == 0:
                        pe.wait_ge(hi_done[c], 5 * n + k + 1)
                    if part == 1:
                        pe.wait_ge(lo_done[c], 5 * n + k + 1)
                    if part == 2 and first:
                        pe.wait_ge(wl1_done, G1 * (k + 1))
                    for i, (g, b) in enumerate(steps):
                        if first and part == 0 and i % KB1 == 0:
                            pe.wait_ge(wh1_done, G1 * k + i // KB1 + 1)
                        block_at = b if c == 1 else KB2 - 1 - b
                        at = (g * KB[c] + block_at) * P
                        (o0, o1), (i0, i1), (u0, u1) = spans(c, j, g, b)
                        ins = nc.tensor.matmul(dst[:, o0:o1, u0:u1], wbuf[c][:, j, at:at + P],
                                               xbuf[c][:, j, i0:i1, g + u0:g + u1],
                                               start=(part == 0 and i == 0),
                                               stop=(part == 2 and i == len(steps) - 1))
                ins.then_inc(conv_mm[c], 1)

            def bank_free(c, n, k, final=False):
                if c == 1:
                    if k < 3:
                        wait(pe, out_done[2], 5 * (n - 2) + (1, 4, 5)[k])
                        if isinstance(n, int) and n == 1:
                            pe.wait_ge(*((m1_read[1], 1), (mid_done[1], 2), (out_done[1], 1))[k])
                    else:
                        wait(pe, out_done[1], 5 * (n - 1) + (4, 5)[k - 3])
                elif k == 0:
                    wait(pe, m1_read[2], n)
                elif k == 1:
                    wait(pe, mid_done[2], 2 * n)
                elif final and k == 2:
                    pe.wait_ge(out_done[2], 5 * (n - 1) + 1)
                elif final:
                    pe.wait_ge(out_done[1], 5 * n + k + 1)
                elif k == 2:
                    pe.wait_ge(m1_read[1], n + 2)
                elif k == 3:
                    pe.wait_ge(mid_done[1], 2 * (n + 2))
                else:
                    pe.wait_ge(out_done[1], 5 * (n + 1) + 1)

            def step(n, prep, ahead, first=False, last=False):
                early = isinstance(n, int) and n < 2
                if not last:
                    for k in range(5):
                        bank_free(1, n, k)
                        conv_stream(1, n, k, first)
                        if k == 2 and first:
                            stats(1, 1)
                        if k == 1 and isinstance(n, int) and n == 1:
                            stats(2, 0)
                        if k == (4 if early else 3) and ahead:
                            stats(1, n + 2)
                if not first:
                    for k in range(5):
                        if isinstance(n, int) and n == 1:
                            parts = W2COUNT[k]
                            pe.wait_ge(wh2_done, parts)
                            pe.wait_ge(wl2_done, parts)
                        bank_free(2, n - 1, k, final=last)
                        conv_stream(2, n - 1, k, final=last)
                        if not last and k == (4 if early else 2 if prep else 0):
                            stats(2, n, shared=not prep)

            pe.wait_ge(tab_loaded, 16)
            stats(1, 0)
            pe.wait_ge(exp_done, G1)
            for _ in range(WARMING):
                nc.tensor.matmul(banks[:, BANK[2][1], 0:P], group_t, group_t, start=True, stop=True)
            step(0, True, True, first=True)
            step(1, True, True)
            with pe.Fori(2, NP - 2) as n:
                step(n, True, True)
            step(NP - 2, True, False)
            step(NP - 1, False, False)
            step(NP, False, False, last=True)


def kernel(x, L0_conv_weight, L0_conv_bias, L1_conv_weight):
    import concourse.bacc as bacc
    from concourse.bass_utils import run_bass_kernel_spmd

    nc = bacc.Bacc("TRN2", target_bir_lowering=False, num_devices=1)
    arrays = {
        "x": np.ascontiguousarray(x),
        "w0": np.ascontiguousarray(L0_conv_weight),
        "bias": np.ascontiguousarray(L0_conv_bias),
        "w1": np.ascontiguousarray(L1_conv_weight),
        "tables": table_constants(),
    }
    args = [nc.dram_tensor(f"in_{k}", a.shape, mybir.dt.from_np(a.dtype), kind="ExternalInput").ap()
            for k, a in arrays.items()]
    out = nc.dram_tensor("out", (B, C, H, W), F32, kind="ExternalOutput").ap()
    build(nc, *args, out)
    r = run_bass_kernel_spmd(nc, [{f"in_{k}": a for k, a in arrays.items()}], core_ids=[0])
    return r.results[0]["out"]
```
